# Optimizing a Trainium2 kernel written in Bass

```python
import numpy as np
import jax
import jax.numpy as jnp

def _softmax(x, axis=-1):
    return jax.nn.softmax(x, axis=axis)

def _gelu(x):
    return jax.nn.gelu(x, approximate=True)

def _silu(x):
    return jax.nn.silu(x)

def _sigmoid(x):
    return jax.nn.sigmoid(x)

def _layernorm(x, axis=-1, eps=1e-05):
    m = jnp.mean(x, axis=axis, keepdims=True)
    v = jnp.var(x, axis=axis, keepdims=True)
    return (x - m) / jnp.sqrt(v + eps)

def _scatter_add(tgt, idx, src, axis=0):
    return tgt.at[idx].add(src)

def _segment_sum(src, seg, n):
    return jax.ops.segment_sum(src, seg, n)
kernel_name = 'mk_xattn_ffn_d1_seqx_r8_833cf3'

def setup_inputs(seed: int=0):
    np.random.seed(seed)
    _w = jnp.asarray

    def _rec_inputs():
        import jax
        import jax.numpy as jnp
        _rk = jax.random.key(seed)
        x = -0.0002928 + 1 * jax.random.normal(jax.random.fold_in(_rk, 1), (8, 100, 128), jnp.float32)
        _lenS = 100 - jax.random.randint(jax.random.fold_in(_rk, 7), (8,), 0, max(1, 100 // 4) + 1, jnp.int32)
        _lenS2 = 1444 - jax.random.randint(jax.random.fold_in(_rk, 8), (8,), 0, max(1, 1444 // 4) + 1, jnp.int32)
        _ctx_1024P = jax.random.normal(jax.random.fold_in(_rk, 11), (8, 16, 128), jnp.float32)
        _ctx_1024c = jax.random.dirichlet(jax.random.fold_in(_rk, 511), 0.3 * jnp.ones((16,), jnp.float32), (8, 1444))
        _ctx_1024t = jnp.einsum('bsk,bkd->bsd', _ctx_1024c, _ctx_1024P)
        _ctx_1024t = _ctx_1024t * jax.lax.rsqrt(jnp.mean(jnp.square(_ctx_1024t)) + 1e-12) * 0.953939
        ctx_1024 = -1.39393e-06 + 0.999914 * (_ctx_1024t + 0.3 * jax.random.normal(jax.random.fold_in(_rk, 611), (8, 1444, 128), jnp.float32))
        _validS = jnp.arange(100)[None, :] < _lenS[:, None]
        _validS2 = jnp.arange(1444)[None, :] < _lenS2[:, None]
        _causal = jnp.tril(jnp.ones((100, 100), dtype=bool))
        mask_BxS2_if1 = jnp.where(jnp.ones((8, 1444), dtype=bool), 1, 0).astype(jnp.int32)
        return (x, ctx_1024, mask_BxS2_if1)
    x, ctx_1024, mask_BxS2_if1 = _rec_inputs()

    def _L0_xattn_setup():
        import jax, jax.numpy as jnp
        import numpy as np
        B, T, D, H = (2, 256, 128, 16)
        DK = D // H
        key = jax.random.key(seed)
        ks = jax.random.split(key, 11)
        w_scale = 1.0 / np.sqrt(D)
        return {'q': jax.random.normal(ks[0], (B, T, D), dtype=jnp.float32), 'k': jax.random.normal(ks[1], (B, T, D), dtype=jnp.float32), 'v': jax.random.normal(ks[2], (B, T, D), dtype=jnp.float32), 'Wq': jax.random.normal(ks[3], (D, D), dtype=jnp.float32) * w_scale, 'bq': jnp.zeros((D,), dtype=jnp.float32), 'Wk': jax.random.normal(ks[4], (D, D), dtype=jnp.float32) * w_scale, 'bk': jnp.zeros((D,), dtype=jnp.float32), 'Wv': jax.random.normal(ks[5], (D, D), dtype=jnp.float32) * w_scale, 'bv': jnp.zeros((D,), dtype=jnp.float32), 'Wo': jax.random.normal(ks[6], (D, D), dtype=jnp.float32) * w_scale, 'bo': jnp.zeros((D,), dtype=jnp.float32), 'mask': jnp.ones((B, T), dtype=jnp.int32), 'causal': 1}
    _L0_xattn_all = _L0_xattn_setup()
    _L0_xattn_in = {k: v for k, v in _L0_xattn_all.items() if k in ('Wq', 'bq', 'Wk', 'bk', 'Wv', 'bv', 'Wo', 'bo')}
    del _L0_xattn_all

    def _L0_ffn_setup():
        import jax, jax.numpy as jnp
        import numpy as np
        B, T, D = (1, 128, 128)
        E, S, H = (8, 2, 512)
        key = jax.random.key(seed)
        kx, kg, k1, k2, k3 = jax.random.split(key, 5)
        X = jax.random.normal(kx, (B, T, D), jnp.float32)
        Wg = jax.random.normal(kg, (D, E), jnp.float32) * 0.02
        bg = jnp.zeros((E,), jnp.float32)
        W1 = jax.random.normal(k1, (E, D, H), jnp.float32) * 0.02
        W3 = jax.random.normal(k3, (E, D, H), jnp.float32) * 0.02
        W2 = jax.random.normal(k2, (E, H, D), jnp.float32) * 0.02
        return {'X': X, 'Wg': Wg, 'bg': bg, 'W1': W1, 'W2': W2, 'W3': W3}
    _L0_ffn_all = _L0_ffn_setup()
    _L0_ffn_in = {k: v for k, v in _L0_ffn_all.items() if k in ('Wg', 'bg', 'W1', 'W2', 'W3')}
    del _L0_ffn_all
    return {'x': x, 'ctx_1024': ctx_1024, 'mask_BxS2_if1': mask_BxS2_if1, 'L0_xattn_Wq': _L0_xattn_in['Wq'], 'L0_xattn_bq': _L0_xattn_in['bq'], 'L0_xattn_Wk': _L0_xattn_in['Wk'], 'L0_xattn_bk': _L0_xattn_in['bk'], 'L0_xattn_Wv': _L0_xattn_in['Wv'], 'L0_xattn_bv': _L0_xattn_in['bv'], 'L0_xattn_Wo': _L0_xattn_in['Wo'], 'L0_xattn_bo': _L0_xattn_in['bo'], 'L0_ffn_Wg': _L0_ffn_in['Wg'], 'L0_ffn_bg': _L0_ffn_in['bg'], 'L0_ffn_W1': _L0_ffn_in['W1'], 'L0_ffn_W2': _L0_ffn_in['W2'], 'L0_ffn_W3': _L0_ffn_in['W3']}

def reference(x, ctx_1024, mask_BxS2_if1, L0_xattn_Wq, L0_xattn_bq, L0_xattn_Wk, L0_xattn_bk, L0_xattn_Wv, L0_xattn_bv, L0_xattn_Wo, L0_xattn_bo, L0_ffn_Wg, L0_ffn_bg, L0_ffn_W1, L0_ffn_W2, L0_ffn_W3):
    import jax
    import jax.numpy as jnp

    def _L0_xattn_ref(q, k, v, Wq, bq, Wk, bk, Wv, bv, Wo, bo, mask, causal):
        import jax, jax.numpy as jnp
        import numpy as np
        B, T, D, H = (2, 256, 128, 16)
        DK = D // H
        Bq, Tq, _ = q.shape
        Tk = k.shape[1]
        qh = (q @ Wq.T + bq).reshape(Bq, Tq, H, DK).transpose(0, 2, 1, 3)
        kh = (k @ Wk.T + bk).reshape(Bq, Tk, H, DK).transpose(0, 2, 1, 3)
        vh = (v @ Wv.T + bv).reshape(Bq, Tk, H, DK).transpose(0, 2, 1, 3)
        logits = jnp.einsum('bhqd,bhkd->bhqk', qh, kh) / jnp.sqrt(jnp.float32(DK))
        neg_inf = jnp.float32(-jnp.inf)
        if causal:
            causal_mask = jnp.tril(jnp.ones((Tq, Tk), dtype=jnp.bool_))
            logits = jnp.where(causal_mask[None, None, :, :], logits, neg_inf)
        if mask is not None:
            logits = jnp.where(mask[:, None, None, :] != 0, logits, neg_inf)
        alphas = jax.nn.softmax(logits, axis=-1)
        context = jnp.einsum('bhqk,bhkd->bhqd', alphas, vh)
        context = context.transpose(0, 2, 1, 3).reshape(Bq, Tq, D)
        return context @ Wo.T + bo

    def _L0_ffn_ref(X, Wg, bg, W1, W2, W3):
        import jax, jax.numpy as jnp
        import numpy as np
        B, T, D = (1, 128, 128)
        E, S, H = (8, 2, 512)
        logits = jnp.einsum('btd,de->bte', X, Wg) + bg
        topv, topi = jax.lax.top_k(logits, S)
        w = jax.nn.softmax(topv, axis=-1)
        xs = X[:, :, None, :] * w[..., None]
        out = X
        for e in range(E):
            h = jax.nn.silu(jnp.einsum('btsd,dh->btsh', xs, W1[e])) * jnp.einsum('btsd,dh->btsh', xs, W3[e])
            y = jnp.einsum('btsh,hd->btsd', h, W2[e])
            mask = (topi == e)[..., None]
            out = out + jnp.where(mask, y, 0.0).sum(axis=2)
        return out
    x = x + _L0_xattn_ref(_layernorm(x, axis=-1), ctx_1024, ctx_1024, L0_xattn_Wq, L0_xattn_bq, L0_xattn_Wk, L0_xattn_bk, L0_xattn_Wv, L0_xattn_bv, L0_xattn_Wo, L0_xattn_bo, mask_BxS2_if1, 1)
    x = x + _L0_ffn_ref(_layernorm(x, axis=-1), L0_ffn_Wg, L0_ffn_bg, L0_ffn_W1, L0_ffn_W2, L0_ffn_W3)
    return x

_drawn_inputs = setup_inputs


def setup_inputs(seed=0):
    import zlib

    import numpy as np

    out = dict(_drawn_inputs(seed))
    spreads = {'L0_xattn_bq': (0.0, 0.325),
     'L0_xattn_bk': (0.0, 0.8),
     'L0_xattn_bv': (0.0, 0.1),
     'L0_xattn_bo': (0.0, 0.1),
     'L0_ffn_bg': (0.0, 0.8)}
    factors = {'L0_ffn_Wg': 8.0, 'L0_ffn_W1': 8.0, 'L0_ffn_W2': 8.0, 'L0_ffn_W3': 8.0}
    for name, (base, spread) in spreads.items():
        noise = np.random.default_rng([zlib.crc32(name.encode()), seed]).standard_normal(out[name].shape)
        drawn = base * np.exp(spread * noise) if base else spread * noise
        out[name] = jnp.asarray(drawn.astype(out[name].dtype))
    for name, factor in factors.items():
        out[name] = (out[name] * factor).astype(out[name].dtype)
    return out
```

```python
from contextlib import ExitStack

import concourse.bass as bass
from concourse import mybir
from concourse.alu_op_type import AluOpType as ALU

ACT = mybir.ActivationFunctionType
AX = mybir.AxisListType
F32 = mybir.dt.float32
F32R = mybir.dt.float32r
BF16 = mybir.dt.bfloat16
I32 = mybir.dt.int32
U32 = mybir.dt.uint32

P = 128
B = 8
T = 100
D = 128
H = 16
DK = D // H
SLABS = H // 4
HG = H // 2
E = 8
F = 512
FC = F // P
WE = 2 * F + FC * D
TOPK = 2
EPS = 1e-5
SCALE = float(DK) ** -0.5
BIG = -1e30
CLAMP = 1e29

R_MH, R_ML, R_KB = 24, 25, 26
V_ONE = DK

SLOT = P
PER_E = (B * T + SLOT - 1) // SLOT * SLOT
TRASH = E * PER_E
ROWS = TRASH + SLOT
TILES = (B * T * TOPK + E * (SLOT - 1)) // SLOT
NJ = PER_E // SLOT
XW = 132


def bass_xattn_moe(nc, x, ctxT, mask, wqkvo, bcols, bo, wg, bg, wffn, out):
    queue = nc.dram_tensor("queue", [ROWS, XW], F32, kind="Internal").ap()
    y_rows = nc.dram_tensor("y_rows", [1 + TOPK * B * T, D], F32, kind="Internal").ap()

    with ExitStack() as st:
        def sb(name, shape, dt=F32):
            return st.enter_context(nc.sbuf_tensor(name, shape, dt))

        def sem(name):
            return st.enter_context(nc.semaphore(name))

        bank = [st.enter_context(nc.psum_tensor(f"bank{i}", [P, 512], F32)) for i in range(8)]

        ident = sb("ident", [P, P])
        identR = sb("identR", [P, P], F32R)
        identB = sb("identB", [P, P], BF16)
        causal = sb("causal", [T, T], BF16)
        before = sb("before", [T, T], BF16)
        onesB = sb("onesB", [T, T], BF16)
        selKH = sb("selKH", [P, SLABS, 4, 4, DK], F32R)
        selKL = sb("selKL", [P, SLABS, 4, 4, DK], F32R)
        selQH = sb("selQH", [P, SLABS, 4, 4, DK], F32R)
        selQL = sb("selQL", [P, SLABS, 4, 4, DK], F32R)
        kbsel = sb("kbsel", [1, 4, 32], F32R)
        part = sb("part", [P, 2], I32)
        rowbias = sb("rowbias", [P, 3])
        mhalf = sb("mhalf", [T, 1])
        expert = sb("expert", [T, E])
        qbase = sb("qbase", [T, E])
        ids = sb("ids", [T, B, TOPK], I32)
        thr = sb("thr", [1, E, NJ])
        upto = sb("upto", [1, E, E])
        tile_no = sb("tile_no", [1, TILES, E])
        tile_row = sb("tile_row", [1, TILES])
        zrow = sb("zrow", [P, 8 * XW])
        xin = sb("xin", [T, B, D])
        xbo = sb("xbo", [T, B, D])
        cxT = sb("cxT", [P, B, T])
        mraw = sb("mraw", [1, B, T], I32)
        kbias = sb("kbias", [1, B, T], F32R)
        w4 = sb("w4", [P, 4, D])
        bc = sb("bc", [P, 3])
        bo_b = sb("bo_b", [T, D])
        bg_b = sb("bg_b", [T, E])
        wg_sb = sb("wg_sb", [P, E])
        wf = sb("wf", [P, E, WE])
        stats = sb("stats", [T, 2, 6])
        mv = sb("mv", [T, 2, 2])
        veps = sb("veps", [T, 2])
        rstd = sb("rstd", [T, 2])
        xn = sb("xn", [T, 2, D])
        xnT = sb("xnT", [P, 2, T])
        kq = sb("kq", [P, 2, T])
        kqh = sb("kqh", [P, 2, T], F32R)
        kql = sb("kql", [P, 2, T], F32R)
        Ks = sb("Ks", [P, 2, SLABS, T], F32R)
        Qs = sb("Qs", [P, 2, SLABS, T], F32R)
        Qa = sb("Qa", [P, 2, SLABS, T], F32R)
        Va = sb("Va", [T, 2, H, 32])
        mx = sb("mx", [T, 4, SLABS])
        mn = sb("mn", [T, 4, SLABS])
        Mp = sb("Mp", [T, 2, SLABS, 4, 32], F32R)
        PT = sb("PT", [T, 2, 4, SLABS, T])
        Tsb = sb("Tsb", [P, 2, SLABS, T])
        rden = sb("rden", [T, H])
        ctxn = sb("ctxn", [T, D])
        coT = sb("coT", [P, T])
        x1 = sb("x1", [T, D])
        stats2 = sb("stats2", [T, 6])
        mv2 = sb("mv2", [T, 2])
        veps2 = sb("veps2", [T, 1])
        rstd2 = sb("rstd2", [T, 1])
        xn2 = sb("xn2", [T, 2, D])
        base = sb("base", [T, B, D])
        xn2T = sb("xn2T", [P, T])
        lg = sb("lg", [T, E])
        top = sb("top", [T, 8])
        topi = sb("topi", [T, 8], U32)
        topf = sb("topf", [T, TOPK])
        dlt = sb("dlt", [T, 1])
        ex = sb("ex", [T, 1])
        den = sb("den", [T, 1])
        wt = sb("wt", [T, 2, TOPK])
        M = sb("M", [T, TOPK, E])
        Ms = sb("Ms", [T, E], BF16)
        Mprev = sb("Mprev", [T, E], BF16)
        r1 = sb("r1", [T, E])
        pr = sb("pr", [T, TOPK, E])
        ps = sb("ps", [T, TOPK])
        pos = sb("pos", [T, 2, TOPK], I32)
        xs = sb("xs", [T, 2, TOPK, XW])
        cmp7 = sb("cmp7", [1, E, NJ])
        tiles = sb("tiles", [1, E])
        tpre = sb("tpre", [1, E, E])
        tend = sb("tend", [1, E])
        cmpt = sb("cmpt", [1, TILES, E])
        tcnt = sb("tcnt", [1, TILES])
        cmps = sb("cmps", [1, TILES, E])
        tst = sb("tst", [1, TILES])
        ta = sb("ta", [1, TILES])
        tb = sb("tb", [1, TILES])
        row_tab = sb("row_tab", [1, TILES], I32)
        exp_tab = sb("exp_tab", [1, TILES], I32)
        xg = sb("xg", [P, 4, XW])
        xgT = sb("xgT", [P, 2, P])
        sg = sb("sg", [P, 2, F])
        hh = sb("hh", [P, 2, F])
        hT = sb("hT", [P, 2, FC, P])
        ysb = sb("ysb", [P, 2, D])
        yin = sb("yin", [T, TOPK, B, D])
        fin = sb("fin", [T, B, D])

        x_in, w_in, b_in, wf_in, zfill = sem("x_in"), sem("w_in"), sem("b_in"), sem("wf_in"), sem("zfill")
        ctx_in = [sem("ctx_in0"), sem("ctx_in1")]
        scat, tile_in, y_out, y_in, o_out = [sem("scat0"), sem("scat1")], sem("tile_in"), sem("y_out"), [sem("y_in0"), sem("y_in1")], sem("o_out")
        tile_ins = [tile_in, sem("tile_in1"), sem("tile_in2"), sem("tile_in3")]
        pool_c, dve_c, c_id = sem("pool_c"), sem("dve_c"), sem("c_id")
        names = ("ln_st ln_ag ln_ve ln_rs xn_r xnT_ps xnT_r q_ps kq_r kqh_r kql_r v_r ksl_ps ksl_r qsl_ps "
                 "qsl_r s1_ps max_r mn_r mh_r ml_r qa_ps qa_r s2_ps exp_r p_r pv_ps t_r tt_ps rd_r cn_r ct_ps "
                 "coT_r wo_ps x1_r l2_st l2_ag l2_ve l2_rs xn2_r x2T_ps x2T_r lg_ps lg_r top_r topi_r topf_r "
                 "dl_r ex_r den_r w1_r w2_r M_r Ms_r mp_r rk_ps r1_r pr_r ps_r pos_r xs_r id_r xbo_r cnt_ps "
                 "tab_s tab_r base_r gT_ps gT_r a_ps b_ps sg_r h_r hT_ps hT_r y_ps ys_r fin_a fin_r").split()
        S = {n: sem(n) for n in names}

        block = st.enter_context(nc.Block())

        def halves(n):
            return n % 2

        @block.sync
        def _(sp):
            sp.dma_start(xin[:], x.rearrange("b t d -> t b d")).then_inc(x_in, 16)
            sp.dma_start(cxT[:, 0:1, :], ctxT[:, 0:1, :]).then_inc(ctx_in[0], 16)
            sp.dma_start(w4[:], wqkvo).then_inc(w_in, 16)
            sp.dma_start(cxT[:, 1:B, :], ctxT[:, 1:B, :]).then_inc(ctx_in[1], 16)
            sp.dma_start(wg_sb[:], wg).then_inc(w_in, 16)
            sp.wait_ge(pool_c, 1)
            zv = queue.rearrange("(p r) c -> p (r c)", p=P)
            per = ROWS // P
            n = 0
            for a in range(0, per, 8):
                k = min(8, per - a)
                sp.dma_start(zv[:, a * XW:(a + k) * XW], zrow[:, 0:k * XW]).then_inc(zfill, 16)
                n += 1
            for e in range(E):
                sp.dma_start(wf[:, e, :], wffn[:, e, :]).then_inc(wf_in, 16)
            sp.wait_ge(scat[0], 16 * TOPK * B // 2)
            sp.wait_ge(scat[1], 16 * TOPK * B // 2)
            sp.wait_ge(S["tab_r"], 2)
            for t in range(TILES):
                if t >= 4:
                    sp.wait_ge(y_out, 16 * (t - 3))
                r = sp.value_load(row_tab[0:1, t:t + 1], min_val=0, max_val=TRASH)
                sp.dma_start(xg[:, t % 4, :], queue[bass.ds(r, SLOT), :]).then_inc(tile_ins[t % 4], 16)
            sp.wait_ge(y_out, 16 * TILES)
            yv = y_rows[1:1 + TOPK * B * T, :].rearrange("(s b t) d -> t s b d", s=TOPK, b=B)
            for c in range(2):
                bs = slice(c * B // 2, (c + 1) * B // 2)
                for s in range(TOPK):
                    sp.dma_start(yin[:, s, bs, :], yv[:, s, bs, :]).then_inc(y_in[c], 16)
            ov = out.rearrange("b t d -> t b d")
            for c in range(2):
                bs = slice(c * B // 2, (c + 1) * B // 2)
                sp.wait_ge(S["fin_r"], c + 1)
                sp.dma_start(ov[:, bs, :], fin[:, bs, :]).then_inc(o_out, 16)
            sp.wait_ge(o_out, 32)

        @block.gpsimd
        def _(g):
            g.memset(zrow[:], 0.0).then_inc(pool_c, 1)
            g.memset(ident[:], 0.0).then_inc(c_id, 1)
            g.wait_ge(c_id, 1)
            g.affine_select(out=ident[:], in_=ident[:], compare_op=ALU.not_equal, fill=1.0, base=0,
                            pattern=[[-1, P]], channel_multiplier=1).then_inc(c_id, 1)
            g.iota(part[:, 0:1], pattern=[[0, 1]], base=0, channel_multiplier=1).then_inc(pool_c, 1)
            g.memset(mhalf[:], -0.5).then_inc(pool_c, 1)
            g.memset(causal[:], 0.0).then_inc(c_id, 1)
            g.memset(onesB[:], 1.0).then_inc(c_id, 1)
            g.wait_ge(c_id, 4)
            g.affine_select(out=causal[:], in_=causal[:], compare_op=ALU.is_ge, fill=BIG, base=0,
                            pattern=[[-1, T]], channel_multiplier=1).then_inc(pool_c, 1)
            g.affine_select(out=before[:], in_=onesB[:], compare_op=ALU.is_gt, fill=0.0, base=0,
                            pattern=[[1, T]], channel_multiplier=-1).then_inc(pool_c, 1)
            g.iota(expert[:], pattern=[[1, E]], base=0, channel_multiplier=0,
                   allow_small_or_imprecise_dtypes=True).then_inc(pool_c, 1)
            g.iota(qbase[:], pattern=[[PER_E, E]], base=-TRASH, channel_multiplier=0,
                   allow_small_or_imprecise_dtypes=True).then_inc(pool_c, 1)
            g.iota(ids[:], pattern=[[T, B], [B * T, TOPK]], base=1, channel_multiplier=1).then_inc(pool_c, 1)
            g.iota(thr[:], pattern=[[0, E], [SLOT, NJ]], base=0, channel_multiplier=0,
                   allow_small_or_imprecise_dtypes=True).then_inc(pool_c, 1)
            g.iota(tile_no[:], pattern=[[1, TILES], [0, E]], base=0, channel_multiplier=0,
                   allow_small_or_imprecise_dtypes=True).then_inc(pool_c, 1)
            g.iota(tile_row[:], pattern=[[SLOT, TILES]], base=0, channel_multiplier=0,
                   allow_small_or_imprecise_dtypes=True).then_inc(pool_c, 1)
            g.memset(upto[:], 1.0).then_inc(c_id, 1)
            g.wait_ge(c_id, 5)
            g.affine_select(out=upto[:], in_=upto[:], compare_op=ALU.is_ge, fill=0.0, base=0,
                            pattern=[[1, E], [-1, E]], channel_multiplier=0).then_inc(pool_c, 1)
            g.dma_start(bc[:], bcols).then_inc(b_in, 16)
            g.dma_start(mraw[:], mask.rearrange("(a b) t -> a b t", a=1)).then_inc(b_in, 16)
            g.dma_start(bo_b[:], bo.rearrange("(a n) -> a n", a=1).broadcast_to([T, D])).then_inc(b_in, 16)
            g.dma_start(bg_b[:], bg.rearrange("(a n) -> a n", a=1).broadcast_to([T, E])).then_inc(b_in, 16)

            def ln1_pow(b):
                g.wait_ge(S["ln_ve"], b + 1)
                g.tensor_tensor(rstd[:, b % 2:b % 2 + 1], veps[:, b % 2:b % 2 + 1], mhalf[:], ALU.pow).then_inc(S["ln_rs"], 1)

            def ln2_pow(b):
                g.wait_ge(S["l2_ve"], b + 1)
                g.tensor_tensor(rstd2[:], veps2[:], mhalf[:], ALU.pow).then_inc(S["l2_rs"], 1)

            def keep_causal(b, u):
                g.wait_ge(S["exp_r"], 2 * b + u + 1)
                v = PT[:, b % 2, 2 * u:2 * u + 2].rearrange("p c s t -> p (c s) t")
                g.affine_select(out=v, in_=v, compare_op=ALU.is_ge, fill=0.0, base=0,
                                pattern=[[0, HG], [1, T]], channel_multiplier=-1).then_inc(S["p_r"], 1)

            def residual(b):
                g.wait_ge(S["xn2_r"], b + 1)
                g.tensor_tensor(base[:, b, :], x1[:], xn2[:, b % 2, :], ALU.add).then_inc(S["base_r"], 1)

            def send(b):
                if b >= 2:
                    g.wait_ge(scat[b % 2], 16 * TOPK * (b // 2))
                g.tensor_copy(xs[:, b % 2, :, D:D + 1].bitcast(I32), ids[:, b, :].unsqueeze(2)).then_inc(S["id_r"], 1)
                g.wait_ge(S["id_r"], b + 1)
                g.wait_ge(S["xs_r"], TOPK * (b + 1))
                g.wait_ge(S["pos_r"], b + 1)
                if b == 0:
                    g.wait_ge(zfill, 16 * ((ROWS // P + 7) // 8))
                for s in range(TOPK):
                    g.indirect_dma_start(queue[:, :], bass.IndirectOffsetOnAxis(ap=pos[:, b % 2, s:s + 1], axis=0),
                                         xs[:, b % 2, s, :], None).then_inc(scat[b % 2], 16)

            g.wait_ge(b_in, 64)
            g.wait_ge(x_in, 16)
            ln1_pow(0)
            for i in range(B + 2):
                if i < B:
                    g.tensor_tensor(xbo[:, i, :], xin[:, i, :], bo_b[:], ALU.add).then_inc(S["xbo_r"], 1)
                if i + 1 < B:
                    ln1_pow(i + 1)
                if 1 <= i <= B:
                    keep_causal(i - 1, 0)
                if 0 <= i - 3:
                    send(i - 3)
                if 1 <= i <= B:
                    keep_causal(i - 1, 1)
                if 0 <= i - 2:
                    ln2_pow(i - 2)
                    residual(i - 2)
            send(B - 1)

            for t in range(TILES):
                g.wait_ge(S["ys_r"], t + 1)
                if t >= 1:
                    g.wait_ge(y_out, 16 * t)
                g.indirect_dma_start(y_rows[:, :], bass.IndirectOffsetOnAxis(ap=xg[:, t % 4, D:D + 1].bitcast(I32), axis=0),
                                     ysb[:, t % 2, :], None).then_inc(y_out, 16)

        @block.scalar
        def _(a):
            a.wait_ge(b_in, 64)
            a.wait_ge(dve_c, 5)

            def xnT_evac(b):
                a.wait_ge(S["xnT_ps"], b + 1)
                a.activation(xnT[:, b % 2, :], bank[6][:, 0:T], ACT.Copy).then_inc(S["xnT_r"], 1)

            def slabs_evac(b):
                a.wait_ge(S["qsl_ps"], b + 1)
                a.activation(Qs[:, b % 2], bank[4][:, 0:SLABS * T].rearrange("p (s t) -> p s t", s=SLABS), ACT.Identity,
                             bias=rowbias[:, 1:2]).then_inc(S["qsl_r"], 1)
                a.wait_ge(S["ksl_ps"], b + 1)
                a.activation(Ks[:, b % 2], bank[6][:, 0:SLABS * T].rearrange("p (s t) -> p s t", s=SLABS), ACT.Identity,
                             bias=rowbias[:, 0:1]).then_inc(S["ksl_r"], 1)

            def qaug_evac(b):
                a.wait_ge(S["qa_ps"], b + 1)
                a.activation(Qa[:, b % 2], bank[4][:, 0:SLABS * T].rearrange("p (s t) -> p s t", s=SLABS), ACT.Identity,
                             bias=rowbias[:, 1:2]).then_inc(S["qa_r"], 1)

            def exps(b, u):
                a.wait_ge(S["s2_ps"], 2 * b + u + 1)
                if b >= 2:
                    a.wait_ge(S["pv_ps"], b - 1)
                for j in range(2):
                    m = a.activation(PT[:, b % 2, 2 * u + j],
                                     bank[2 + j][0:T, 0:SLABS * T].rearrange("p (s t) -> p s t", s=SLABS), ACT.Exp,
                                     scale=SCALE)
                m.then_inc(S["exp_r"], 1)

            def t_evac(b):
                a.wait_ge(S["pv_ps"], b + 1)
                a.activation(Tsb[:, b % 2], bank[5][:, 0:SLABS * T].rearrange("p (s t) -> p s t", s=SLABS),
                             ACT.Copy).then_inc(S["t_r"], 1)

            def coT_evac(b):
                a.wait_ge(S["ct_ps"], b + 1)
                a.activation(coT[:], bank[7][:, 0:T], ACT.Identity, bias=bc[:, 2:3]).then_inc(S["coT_r"], 1)

            def route(b):
                a.wait_ge(S["dl_r"], b + 1)
                a.activation(ex[:], dlt[:], ACT.Exp).then_inc(S["ex_r"], 1)

            def scale_rows(b):
                a.wait_ge(S["w2_r"], b + 1)
                if b >= 2:
                    a.wait_ge(scat[b % 2], 16 * TOPK * (b // 2))
                for s in range(TOPK):
                    a.activation(xs[:, b % 2, s, 0:D], xn2[:, b % 2, :], ACT.Copy,
                                 scale=wt[:, b % 2, s:s + 1]).then_inc(S["xs_r"], 1)

            xnT_evac(0)
            slabs_evac(0)
            for i in range(B + 2):
                if 1 <= i <= B:
                    exps(i - 1, 0)
                if i + 1 < B:
                    xnT_evac(i + 1)
                if 1 <= i <= B:
                    exps(i - 1, 1)
                if i < B:
                    qaug_evac(i)
                if 0 <= i - 2:
                    coT_evac(i - 2)
                if 1 <= i <= B:
                    t_evac(i - 1)
                if i + 1 < B:
                    slabs_evac(i + 1)
                if 0 <= i - 2:
                    route(i - 2)
                    scale_rows(i - 2)

            def silu(t):
                a.wait_ge(S["a_ps"], t + 1)
                if t >= 2:
                    a.wait_ge(S["h_r"], t - 1)
                a.activation(sg[:, t % 2, :], bank[1 + t % 2][:], ACT.Silu).then_inc(S["sg_r"], 1)

            def hT_evac(t):
                a.wait_ge(S["hT_ps"], t + 1)
                if t >= 2:
                    a.wait_ge(S["y_ps"], t - 1)
                a.activation(hT[:, t % 2], bank[5 + t % 2][:].rearrange("p (c t) -> p c t", c=FC),
                             ACT.Copy).then_inc(S["hT_r"], 1)

            silu(0)
            for t in range(TILES):
                if t + 1 < TILES:
                    silu(t + 1)
                hT_evac(t)

        @block.tensor
        def _(pe):
            pe.wait_ge(c_id, 2)
            pe.wait_ge(dve_c, 5)
            pe.wait_ge(pool_c, 12)

            def xn_turn(b):
                if b >= 1:
                    pe.wait_ge(S["ksl_r"], b)
                pe.wait_ge(S["xn_r"], b + 1)
                pe.transpose(bank[6][:, 0:T], xn[:, b % 2, :], ident[0:T, 0:T]).then_inc(S["xnT_ps"], 1)

            def kv(b):
                if b < 2:
                    pe.wait_ge(ctx_in[b], 16)
                    pe.wait_ge(w_in, 32)
                pe.wait_ge(S["xnT_r"], b + 1)
                pe.matmul(bank[6][:, T:2 * T], w4[:, 1, :], cxT[:, b, :], start=True, stop=True)
                pe.matmul(bank[6][0:T, 3 * T:3 * T + D], cxT[:, b, :], w4[:, 2, :], start=True,
                          stop=True)

            def q(b):
                pe.wait_ge(S["xnT_r"], b + 1)
                pe.matmul(bank[6][:, 2 * T:3 * T], w4[:, 0, :], xnT[:, b % 2, :], start=True,
                          stop=True).then_inc(S["q_ps"], 1)

            def slabs(b):
                pe.wait_ge(S["kql_r"], b + 1)
                pe.wait_ge(S["v_r"], b + 1)
                if b >= 1:
                    pe.wait_ge(S["qa_r"], b)
                for s in range(SLABS):
                    o = bank[4][:, s * T:(s + 1) * T]
                    pe.matmul(o, selQH[:, s].rearrange("p c j d -> p (c j d)"), kqh[:, 1, :], start=(s == 0),
                              stop=False, skip_group_check=True)
                    m = pe.matmul(o, selQL[:, s].rearrange("p c j d -> p (c j d)"), kql[:, 1, :], start=False,
                                  stop=False, skip_group_check=True)
                m.then_inc(S["qsl_ps"], 1)
                for s in range(SLABS):
                    o = bank[6][:, s * T:(s + 1) * T]
                    pe.matmul(o, selKH[:, s].rearrange("p c j d -> p (c j d)"), kqh[:, 0, :], start=True,
                              stop=False, skip_group_check=True)
                    pe.matmul(o, selKL[:, s].rearrange("p c j d -> p (c j d)"), kql[:, 0, :], start=False,
                              stop=False, skip_group_check=True)
                    m = pe.matmul(o, kbsel[:].rearrange("p c r -> p (c r)"), kbias[:, b, :], start=False,
                                  stop=True, skip_group_check=True)
                m.then_inc(S["ksl_ps"], 1)

            def s1(b, u):
                if u == 0:
                    pe.wait_ge(S["ksl_r"], b + 1)
                for j in range(2):
                    n = 2 * (2 * b + u) + j
                    if n >= 2:
                        pe.wait_ge(S["max_r"], n - 1)
                    pe.matmul(bank[j][0:T, 0:4 * T].rearrange("p (s t) -> p s t", s=SLABS), identB[0:T, 0:T],
                              causal[:].unsqueeze(1).broadcast_to([T, SLABS, T]), start=True, stop=False,
                              skip_group_check=True)
                for s in range(SLABS):
                    for j in range(2):
                        r = slice(32 * (2 * u + j), 32 * (2 * u + j) + 32)
                        m = pe.matmul(bank[j][0:T, s * T:(s + 1) * T], Qs[r, b % 2, s, :], Ks[r, b % 2, s, :],
                                      start=False, stop=True, skip_group_check=True)
                        if s == SLABS - 1:
                            m.then_inc(S["s1_ps"], 1)

            def place_max(b):
                pe.wait_ge(S["ml_r"], b + 1)
                for s in range(SLABS):
                    m = pe.matmul(bank[4][:, s * T:(s + 1) * T], Mp[:, b % 2, s].rearrange("p c r -> p (c r)"),
                                  identR[0:T, 0:T], start=False, stop=True, skip_group_check=True)
                m.then_inc(S["qa_ps"], 1)

            def s2(b, u):
                pe.wait_ge(S["qa_r"], b + 1)
                if 2 * b + u >= 1:
                    pe.wait_ge(S["exp_r"], 2 * b + u)
                for s in range(SLABS):
                    for j in range(2):
                        r = slice(32 * (2 * u + j), 32 * (2 * u + j) + 32)
                        m = pe.matmul(bank[2 + j][0:T, s * T:(s + 1) * T], Ks[r, b % 2, s, :], Qa[r, b % 2, s, :],
                                      start=True, stop=True)
                m.then_inc(S["s2_ps"], 1)

            def pv(b):
                if b >= 2:
                    pe.wait_ge(S["r1_r"], b - 1)
                pe.wait_ge(S["p_r"], 2 * b + 2)
                for s in range(SLABS):
                    for c in range(4):
                        m = pe.matmul(bank[5][32 * c:32 * c + 32, s * T:(s + 1) * T], Va[:, b % 2, 4 * s + c, :],
                                      PT[:, b % 2, c, s, :], start=True, stop=True)
                m.then_inc(S["pv_ps"], 1)

            def t_turn(b):
                pe.wait_ge(S["t_r"], b + 1)
                if b >= 1:
                    pe.wait_ge(S["x1_r"], b)
                for s in range(SLABS):
                    m = pe.transpose(bank[7][0:T, s * P:(s + 1) * P], Tsb[:, b % 2, s, :], ident[:])
                m.then_inc(S["tt_ps"], 1)

            def ctx_turn(b):
                pe.wait_ge(S["cn_r"], b + 1)
                pe.transpose(bank[7][:, 0:T], ctxn[:], ident[0:T, 0:T]).then_inc(S["ct_ps"], 1)

            def wo(b):
                pe.wait_ge(S["coT_r"], b + 1)
                pe.matmul(bank[7][0:T, P:P + D], coT[:], w4[:, 3, :], start=True, stop=True).then_inc(S["wo_ps"], 1)

            def xn2_turn(b):
                pe.wait_ge(S["xn2_r"], b + 1)
                pe.wait_ge(S["t_r"], min(b + 2, B))
                pe.transpose(bank[5][:, 0:T], xn2[:, b % 2, :], ident[0:T, 0:T]).then_inc(S["x2T_ps"], 1)

            def logits(b):
                pe.wait_ge(S["x2T_r"], b + 1)
                pe.matmul(bank[5][0:T, 0:E], xn2T[:], wg_sb[:], start=True, stop=True).then_inc(S["lg_ps"], 1)

            def rank(b):
                pe.wait_ge(S["Ms_r"], b + 1)
                pe.wait_ge(S["mp_r"], b + 1)
                if b >= 1:
                    pe.wait_ge(S["r1_r"], b)
                pe.matmul(bank[5][0:T, 0:E], before[:], Ms[:], start=True, stop=False)
                pe.matmul(bank[5][0:T, 0:E], onesB[:], Mprev[:], start=False, stop=True).then_inc(S["rk_ps"], 1)

            xn_turn(0)
            kv(0)
            q(0)
            slabs(0)
            for i in range(B + 2):
                if i < B:
                    s1(i, 0)
                if 1 <= i <= B:
                    s2(i - 1, 0)
                if i < B:
                    s1(i, 1)
                if 1 <= i <= B:
                    s2(i - 1, 1)
                if i + 1 < B:
                    xn_turn(i + 1)
                if 0 <= i - 2:
                    t_turn(i - 2)
                if i + 1 < B:
                    kv(i + 1)
                    q(i + 1)
                if i < B:
                    place_max(i)
                if 0 <= i - 2:
                    ctx_turn(i - 2)
                if 1 <= i <= B:
                    pv(i - 1)
                if 0 <= i - 2:
                    wo(i - 2)
                if i + 1 < B:
                    slabs(i + 1)
                if 0 <= i - 2:
                    xn2_turn(i - 2)
                    logits(i - 2)
                    rank(i - 2)
            pe.wait_ge(S["mp_r"], B + 1)
            pe.matmul(bank[5][0:T, 0:E], onesB[:], Mprev[:], start=True, stop=True).then_inc(S["cnt_ps"], 1)

            def x_turn(t):
                pe.wait_ge(tile_ins[t % 4], 16 * (t // 4 + 1))
                if t >= 1:
                    pe.wait_ge(S["gT_r"], t)
                pe.transpose(bank[0][:, 0:P], xg[:, t % 4, 0:D], ident[:]).then_inc(S["gT_ps"], 1)

            def up(t):
                pe.wait_ge(S["gT_r"], t + 1)
                if t >= 2:
                    pe.wait_ge(S["sg_r"], t - 1)
                e = pe.value_load(exp_tab[0:1, t:t + 1], min_val=0, max_val=(E - 1) * WE)
                wrow = wf[:].rearrange("p e n -> p (e n)")
                pe.matmul(bank[1 + t % 2][:], xgT[:, t % 2, :], wrow[:, bass.ds(e, F)], start=True, stop=True)\
                    .then_inc(S["a_ps"], 1)
                if t >= 1:
                    pe.wait_ge(S["h_r"], t)
                pe.matmul(bank[3][:], xgT[:, t % 2, :], wrow[:, bass.ds(e + F, F)], start=True, stop=True)\
                    .then_inc(S["b_ps"], 1)
                return e, wrow

            def h_turn(t):
                pe.wait_ge(S["h_r"], t + 1)
                if t >= 2:
                    pe.wait_ge(S["hT_r"], t - 1)
                for c in range(FC):
                    m = pe.transpose(bank[5 + t % 2][:, c * P:(c + 1) * P], hh[:, t % 2, c * P:(c + 1) * P], ident[:])
                m.then_inc(S["hT_ps"], 1)

            def down(t, e, wrow):
                pe.wait_ge(S["hT_r"], t + 1)
                if t >= 2:
                    pe.wait_ge(S["ys_r"], t - 1)
                for c in range(FC):
                    m = pe.matmul(bank[4 + 3 * (t % 2)][:, 0:D], hT[:, t % 2, c, :],
                                  wrow[:, bass.ds(e + 2 * F + c * D, D)], start=(c == 0), stop=(c == FC - 1))
                m.then_inc(S["y_ps"], 1)

            pe.wait_ge(wf_in, 16 * E)
            pe.wait_ge(S["tab_r"], 2)
            x_turn(0)
            cur = up(0)
            x_turn(1)
            for t in range(TILES):
                nxt = up(t + 1) if t + 1 < TILES else None
                h_turn(t)
                if t + 2 < TILES:
                    x_turn(t + 2)
                down(t, *cur)
                cur = nxt

        @block.vector
        def _(v):
            v.memset(selKH[:].bitcast(U32), 0)
            v.memset(selKL[:].bitcast(U32), 0)
            v.memset(selQH[:].bitcast(U32), 0)
            v.memset(selQL[:].bitcast(U32), 0)
            v.memset(kbsel[:].bitcast(U32), 0)
            v.memset(Va[:], 0.0)
            v.memset(Mp[:].bitcast(U32), 0)
            v.memset(xs[:], 0.0)
            v.memset(Mprev[:], 0.0).then_inc(dve_c, 1)
            v.wait_ge(c_id, 2)
            v.wait_ge(dve_c, 1)
            iv = ident[:].rearrange("p (s c d) -> p s c d", s=SLABS, c=4)
            for sel, js in ((selKH, (0, 2)), (selKL, (1,)), (selQH, (0, 1)), (selQL, (2,))):
                for j in js:
                    v.tensor_copy(sel[:, :, :, j, :], iv)
            v.memset(Va[:, :, :, V_ONE:V_ONE + 1], 1.0)
            v.tensor_copy(identR[:], ident[:])
            v.tensor_copy(identB[:], ident[:]).then_inc(dve_c, 1)
            v.tensor_scalar(kbsel[:, :, R_KB:R_KB + 1], kbsel[:, :, R_KB:R_KB + 1].bitcast(F32), 1.0, None, ALU.add)
            v.wait_ge(pool_c, 3)
            v.tensor_scalar(part[:, 1:2], part[:, 0:1], 31, None, ALU.bitwise_and).then_inc(dve_c, 1)
            v.wait_ge(dve_c, 3)
            v.tensor_scalar(rowbias[:, 1:2], part[:, 1:2], float(R_KB), None, ALU.is_equal)
            v.tensor_scalar(rowbias[:, 2:3], part[:, 1:2], float(R_MH), None, ALU.is_ge).then_inc(dve_c, 1)
            v.wait_ge(dve_c, 4)
            v.scalar_tensor_tensor(rowbias[:, 0:1], part[:, 1:2], float(R_ML), rowbias[:, 2:3], ALU.is_le, ALU.mult)
            v.wait_ge(b_in, 64)
            v.tensor_scalar(kbias[:], mraw[:], 0.0, BIG, ALU.is_equal, ALU.mult).then_inc(dve_c, 1)

            def ln1(b):
                v.bn_stats(stats[:, b % 2, :], xin[:, b, :]).then_inc(S["ln_st"], 1)
                v.wait_ge(S["ln_st"], b + 1)
                v.bn_aggr(mv[:, b % 2, :], stats[:, b % 2, :]).then_inc(S["ln_ag"], 1)
                v.wait_ge(S["ln_ag"], b + 1)
                v.tensor_scalar(veps[:, b % 2:b % 2 + 1], mv[:, b % 2, 1:2], EPS, None, ALU.add).then_inc(S["ln_ve"], 1)

            def ln1_apply(b):
                v.wait_ge(S["ln_rs"], b + 1)
                v.tensor_scalar(xn[:, b % 2, :], xin[:, b, :], mv[:, b % 2, 0:1], rstd[:, b % 2:b % 2 + 1],
                                ALU.subtract, ALU.mult).then_inc(S["xn_r"], 1)

            def v_evac(b):
                v.wait_ge(S["q_ps"], b + 1)
                if b >= 2:
                    v.wait_ge(S["pv_ps"], b - 1)
                v.tensor_copy(Va[:, b % 2, :, 0:DK],
                              bank[6][0:T, 3 * T:3 * T + D].rearrange("p (h d) -> p h d", h=H)).then_inc(S["v_r"], 1)

            def kq_split(b):
                v.wait_ge(S["q_ps"], b + 1)
                if b >= 1:
                    v.wait_ge(S["ksl_ps"], b)
                v.tensor_tensor(kq[:], bank[6][:, T:3 * T].rearrange("p (w t) -> p w t", w=2),
                                bc[:, 0:2].unsqueeze(2).broadcast_to([P, 2, T]), ALU.add).then_inc(S["kq_r"], 1)
                v.wait_ge(S["kq_r"], b + 1)
                v.tensor_copy(kqh[:], kq[:]).then_inc(S["kqh_r"], 1)
                v.wait_ge(S["kqh_r"], b + 1)
                v.tensor_tensor(kql[:], kq[:], kqh[:].bitcast(F32), ALU.subtract).then_inc(S["kql_r"], 1)

            def maxima(b, u):
                for j in range(2):
                    n = 2 * (2 * b + u) + j
                    v.wait_ge(S["s1_ps"], n + 1)
                    v.tensor_reduce(mx[:, 2 * u + j], bank[j][0:T, 0:SLABS * T].rearrange("p (s t) -> p s t", s=SLABS),
                                    AX.X, ALU.max).then_inc(S["max_r"], 1)

            def negate_max(b):
                v.wait_ge(S["max_r"], 4 * b + 4)
                v.tensor_scalar(mn[:], mx[:], -1.0, CLAMP, ALU.mult, ALU.min).then_inc(S["mn_r"], 1)
                v.wait_ge(S["mn_r"], b + 1)
                mp = Mp[:, b % 2].rearrange("p s c r -> p c s r")
                v.tensor_copy(mp[:, :, :, R_MH], mn[:]).then_inc(S["mh_r"], 1)
                v.wait_ge(S["mh_r"], b + 1)
                v.tensor_tensor(mp[:, :, :, R_ML], mn[:], mp[:, :, :, R_MH].bitcast(F32), ALU.subtract)\
                    .then_inc(S["ml_r"], 1)

            def norm(b):
                v.wait_ge(S["tt_ps"], b + 1)
                o = bank[7][0:T, :].rearrange("p (h r) -> p h r", h=H)
                v.reciprocal(rden[:], o[:, :, V_ONE]).then_inc(S["rd_r"], 1)
                v.wait_ge(S["rd_r"], b + 1)
                v.tensor_tensor(ctxn[:].rearrange("p (h d) -> p h d", h=H), o[:, :, 0:DK],
                                rden[:].unsqueeze(2).broadcast_to([T, H, DK]), ALU.mult).then_inc(S["cn_r"], 1)

            def ln2(b):
                v.wait_ge(S["wo_ps"], b + 1)
                v.wait_ge(S["xbo_r"], b + 1)
                if b >= 1:
                    v.wait_ge(S["base_r"], b)
                v.tensor_tensor(x1[:], bank[7][0:T, P:P + D], xbo[:, b, :], ALU.add).then_inc(S["x1_r"], 1)
                v.wait_ge(S["x1_r"], b + 1)
                v.bn_stats(stats2[:], x1[:]).then_inc(S["l2_st"], 1)
                v.wait_ge(S["l2_st"], b + 1)
                v.bn_aggr(mv2[:], stats2[:]).then_inc(S["l2_ag"], 1)
                v.wait_ge(S["l2_ag"], b + 1)
                v.tensor_scalar(veps2[:], mv2[:, 1:2], EPS, None, ALU.add).then_inc(S["l2_ve"], 1)

            def ln2_apply(b):
                v.wait_ge(S["l2_rs"], b + 1)
                if b >= 2:
                    v.wait_ge(S["xs_r"], TOPK * (b - 1))
                v.tensor_scalar(xn2[:, b % 2, :], x1[:], mv2[:, 0:1], rstd2[:], ALU.subtract, ALU.mult)\
                    .then_inc(S["xn2_r"], 1)

            def xn2T_evac(b):
                v.wait_ge(S["x2T_ps"], b + 1)
                if b >= 1:
                    v.wait_ge(S["lg_ps"], b)
                v.tensor_copy(xn2T[:], bank[5][:, 0:T]).then_inc(S["x2T_r"], 1)

            def choose(b):
                v.wait_ge(S["lg_ps"], b + 1)
                v.tensor_tensor(lg[:], bank[5][0:T, 0:E], bg_b[:], ALU.add).then_inc(S["lg_r"], 1)
                v.wait_ge(S["lg_r"], b + 1)
                v.max(top[:], lg[:]).then_inc(S["top_r"], 1)
                v.wait_ge(S["top_r"], b + 1)
                v.max_index(topi[:], top[:], lg[:]).then_inc(S["topi_r"], 1)
                v.tensor_tensor(dlt[:], top[:, 1:2], top[:, 0:1], ALU.subtract).then_inc(S["dl_r"], 1)
                v.wait_ge(S["topi_r"], b + 1)
                v.tensor_copy(topf[:], topi[:, 0:TOPK]).then_inc(S["topf_r"], 1)
                v.wait_ge(S["topf_r"], b + 1)
                v.tensor_tensor(M[:], expert[:].unsqueeze(1).broadcast_to([T, TOPK, E]),
                                topf[:].unsqueeze(2).broadcast_to([T, TOPK, E]), ALU.is_equal).then_inc(S["M_r"], 1)
                v.wait_ge(S["M_r"], b + 1)
                if b >= 1:
                    v.wait_ge(S["rk_ps"], b)
                    v.tensor_tensor(Mprev[:], Mprev[:], Ms[:], ALU.add).then_inc(S["mp_r"], 1)
                    v.wait_ge(S["mp_r"], b + 1)
                else:
                    v.memset(Mprev[:], 0.0).then_inc(S["mp_r"], 1)
                v.tensor_tensor(Ms[:], M[:, 0, :], M[:, 1, :], ALU.add).then_inc(S["Ms_r"], 1)
                v.wait_ge(S["ex_r"], b + 1)
                v.tensor_scalar(den[:], ex[:], 1.0, None, ALU.add).then_inc(S["den_r"], 1)
                v.wait_ge(S["den_r"], b + 1)
                if b >= 2:
                    v.wait_ge(S["xs_r"], TOPK * (b - 1))
                v.reciprocal(wt[:, b % 2, 0:1], den[:]).then_inc(S["w1_r"], 1)
                v.wait_ge(S["w1_r"], b + 1)
                v.tensor_tensor(wt[:, b % 2, 1:2], ex[:], wt[:, b % 2, 0:1], ALU.mult).then_inc(S["w2_r"], 1)

            def place(b):
                v.wait_ge(S["rk_ps"], b + 1)
                v.tensor_tensor(r1[:], bank[5][0:T, 0:E], qbase[:], ALU.add).then_inc(S["r1_r"], 1)
                v.wait_ge(S["r1_r"], b + 1)
                v.tensor_tensor(pr[:], M[:], r1[:].unsqueeze(1).broadcast_to([T, TOPK, E]), ALU.mult)\
                    .then_inc(S["pr_r"], 1)
                v.wait_ge(S["pr_r"], b + 1)
                v.tensor_reduce(ps[:], pr[:], AX.X, ALU.add).then_inc(S["ps_r"], 1)
                v.wait_ge(S["ps_r"], b + 1)
                if b >= 2:
                    v.wait_ge(scat[b % 2], 16 * TOPK * (b // 2))
                v.tensor_scalar(pos[:, b % 2, :], ps[:], float(TRASH), None, ALU.add).then_inc(S["pos_r"], 1)

            v.wait_ge(x_in, 16)
            v.wait_ge(pool_c, 12)
            ln1(0)
            ln1_apply(0)
            v_evac(0)
            kq_split(0)
            for i in range(B + 2):
                if i + 1 < B:
                    ln1(i + 1)
                if i < B:
                    maxima(i, 0)
                if i + 1 < B:
                    ln1_apply(i + 1)
                if i < B:
                    maxima(i, 1)
                    negate_max(i)
                if 0 <= i - 2:
                    norm(i - 2)
                    ln2(i - 2)
                if i + 1 < B:
                    v_evac(i + 1)
                    kq_split(i + 1)
                if 0 <= i - 2:
                    ln2_apply(i - 2)
                    xn2T_evac(i - 2)
                    choose(i - 2)
                    place(i - 2)
            v.tensor_tensor(Mprev[:], Mprev[:], Ms[:], ALU.add).then_inc(S["mp_r"], 1)
            tab = [0]

            def link(ins):
                tab[0] += 1
                ins.then_inc(S["tab_s"], 1)
                v.wait_ge(S["tab_s"], tab[0])

            v.wait_ge(S["cnt_ps"], 1)
            link(v.tensor_tensor(cmp7[:], bank[5][0:1, 0:E].unsqueeze(2).broadcast_to([1, E, NJ]), thr[:], ALU.is_gt))
            link(v.tensor_reduce(tiles[:], cmp7[:], AX.X, ALU.add))
            link(v.tensor_tensor(tpre[:], tiles[:].unsqueeze(1).broadcast_to([1, E, E]), upto[:], ALU.mult))
            link(v.tensor_reduce(tend[:], tpre[:], AX.X, ALU.add))
            link(v.tensor_tensor(cmpt[:], tend[:].unsqueeze(1).broadcast_to([1, TILES, E]), tile_no[:], ALU.is_le))
            link(v.tensor_reduce(tcnt[:], cmpt[:], AX.X, ALU.add))
            link(v.tensor_scalar(exp_tab[:], tcnt[:], float(E - 1), float(WE), ALU.min, ALU.mult))
            link(v.tensor_tensor(cmps[:], tiles[:].unsqueeze(1).broadcast_to([1, TILES, E]), cmpt[:], ALU.mult))
            link(v.tensor_reduce(tst[:], cmps[:], AX.X, ALU.add))
            link(v.scalar_tensor_tensor(ta[:], tst[:], -float(SLOT), tile_row[:], ALU.mult, ALU.add))
            link(v.scalar_tensor_tensor(tb[:], tcnt[:], float(PER_E), ta[:], ALU.mult, ALU.add))
            v.tensor_scalar(row_tab[:], tb[:], float(TRASH), None, ALU.min).then_inc(S["tab_r"], 2)

            def gT_evac(t):
                v.wait_ge(S["gT_ps"], t + 1)
                if t >= 2:
                    v.wait_ge(S["b_ps"], t - 1)
                v.tensor_copy(xgT[:, t % 2, :], bank[0][:, 0:P]).then_inc(S["gT_r"], 1)

            def gate(t):
                v.wait_ge(S["sg_r"], t + 1)
                v.wait_ge(S["b_ps"], t + 1)
                if t >= 2:
                    v.wait_ge(S["hT_ps"], t - 1)
                v.tensor_tensor(hh[:, t % 2, :], sg[:, t % 2, :], bank[3][:], ALU.mult).then_inc(S["h_r"], 1)

            def y_evac(t):
                v.wait_ge(S["y_ps"], t + 1)
                if t >= 2:
                    v.wait_ge(y_out, 16 * (t - 1))
                v.tensor_copy(ysb[:, t % 2, :], bank[4 + 3 * (t % 2)][:, 0:D]).then_inc(S["ys_r"], 1)

            gT_evac(0)
            gate(0)
            gT_evac(1)
            for t in range(TILES):
                if t + 1 < TILES:
                    gate(t + 1)
                if t + 2 < TILES:
                    gT_evac(t + 2)
                y_evac(t)
            for c in range(2):
                bs = slice(c * B // 2, (c + 1) * B // 2)
                v.wait_ge(y_in[c], 16 * TOPK)
                v.wait_ge(S["base_r"], B)
                v.tensor_tensor(fin[:, bs, :], yin[:, 0, bs, :], yin[:, 1, bs, :], ALU.add).then_inc(S["fin_a"], 1)
                v.wait_ge(S["fin_a"], c + 1)
                v.tensor_tensor(fin[:, bs, :], fin[:, bs, :], base[:, bs, :], ALU.add).then_inc(S["fin_r"], 1)


def kernel(**inputs):
    import numpy as np
    import concourse.bacc as bacc
    from concourse.bass_utils import run_bass_kernel_spmd

    i = {k: np.asarray(v) for k, v in inputs.items()}
    w = [i["L0_xattn_" + n] for n in ("Wq", "Wk", "Wv", "Wo")]
    e13 = np.stack([i["L0_ffn_W1"], i["L0_ffn_W3"]], axis=2)
    e2 = i["L0_ffn_W2"].reshape(E, FC, P, D).transpose(2, 0, 1, 3)
    arrays = {
        "x": i["x"],
        "ctxT": i["ctx_1024"][:, :T, :].transpose(2, 0, 1),
        "mask": i["mask_BxS2_if1"][:, :T],
        "wqkvo": np.stack([a.T for a in w], axis=1),
        "bcols": np.stack([i["L0_xattn_bk"], i["L0_xattn_bq"], i["L0_xattn_bv"]], axis=1),
        "bo": i["L0_xattn_bo"],
        "wg": i["L0_ffn_Wg"],
        "bg": i["L0_ffn_bg"],
        "wffn": np.concatenate([e13.transpose(1, 0, 2, 3).reshape(P, E, 2 * F), e2.reshape(P, E, FC * D)], axis=2),
    }
    arrays = {k: np.ascontiguousarray(a) for k, a in arrays.items()}
    nc = bacc.Bacc("TRN2", target_bir_lowering=False, num_devices=1)
    args = [nc.dram_tensor(k, a.shape, mybir.dt.from_np(a.dtype), kind="ExternalInput").ap() for k, a in arrays.items()]
    args.append(nc.dram_tensor("out", (B, T, D), F32, kind="ExternalOutput").ap())
    bass_xattn_moe(nc, *args)
    r = run_bass_kernel_spmd(nc, [arrays], core_ids=[0])
    return r.results[0]["out"]
```

```python
from contextlib import ExitStack

import concourse.bass as bass
from concourse import mybir
from concourse.alu_op_type import AluOpType as ALU

ACT = mybir.ActivationFunctionType
AX = mybir.AxisListType
F32 = mybir.dt.float32
F32R = mybir.dt.float32r
BF16 = mybir.dt.bfloat16
I32 = mybir.dt.int32
U32 = mybir.dt.uint32

P = 128
B = 8
T = 100
D = 128
H = 16
DK = D // H
SLABS = H // 4
HG = H // 2
E = 8
F = 512
FC = F // P
WE = 2 * F + FC * D
TOPK = 2
EPS = 1e-5
SCALE = float(DK) ** -0.5
BIG = -1e30
CLAMP = 1e29

R_MH, R_ML, R_KB = 24, 25, 26
V_ONE = DK

SLOT = P
PER_E = (B * T + SLOT - 1) // SLOT * SLOT
TRASH = E * PER_E
ROWS = TRASH + SLOT
TILES = (B * T * TOPK + E * (SLOT - 1)) // SLOT
NJ = PER_E // SLOT
RING = 8

CH = B // 2
CT = CH * T
STEPS = [("K", 0, "A"), ("xT", 0, "A"), ("Q", 0, "A")] + [("Ks", s, "A") for s in range(SLABS)]
STEPS += [("Qs", s, "V" if s % 2 else "A") for s in range(SLABS)] + [("V", 0, "V"), ("V", 1, "V")]
NSTEP = len(STEPS)


def step_bank(n):
    return n % 4 if n < NSTEP - 2 else (5, 7, 5, 6, 7, 5, 6, 7, 5, 6, 7, 6, 7, 6, 6)[n - (NSTEP - 2)]


def step_before(n):
    had = [m for m in range(n) if step_bank(m) == step_bank(n)]
    return had[-1] if had else None


def taken_out(n):
    eng = STEPS[n % NSTEP][2]
    return eng, sum(STEPS[m % NSTEP][2] == eng for m in range(n + 1))


EARLY = {0: STEPS[0:3], 1: STEPS[7:9]}
LATE = {0: STEPS[3:7], 1: STEPS[9:11], 2: STEPS[11:13]}

SPREADS = {1: (2, 3), 2: (4, 5), 3: (6,), 4: (7,)}


def step_no(g, kind, k=0):
    return g * NSTEP + [(a, b) for a, b, _ in STEPS].index((kind, k))

XW = D + 1
ZR = WE // XW
NZ = (ROWS // P + ZR - 1) // ZR


def bass_xattn_moe(nc, x, ctxT, mask, wqkvo, bcols, bo, wg, bg, wffn, out):
    queue = nc.dram_tensor("queue", [ROWS, XW], F32, kind="Internal").ap()
    y_rows = nc.dram_tensor("y_rows", [2 + TOPK * B * T, D], F32, kind="Internal").ap()

    with ExitStack() as st:
        def sb(name, shape, dt=F32):
            return st.enter_context(nc.sbuf_tensor(name, shape, dt))

        def sem(name):
            return st.enter_context(nc.semaphore(name))

        bank = [st.enter_context(nc.psum_tensor(f"bank{i}", [P, 512], F32)) for i in range(8)]

        ident = sb("ident", [P, P])
        identR = sb("identR", [P, P], F32R)
        identB = sb("identB", [P, P], BF16)
        causal = sb("causal", [P, T], BF16)
        before = sb("before", [T, T], BF16)
        onesB = sb("onesB", [T, T], BF16)
        selKH = sb("selKH", [P, SLABS, 4, 4, DK], F32R)
        selKL = sb("selKL", [P, SLABS, 4, 4, DK], F32R)
        selQH = sb("selQH", [P, SLABS, 4, 4, DK], F32R)
        selQL = sb("selQL", [P, SLABS, 4, 4, DK], F32R)
        kbsel = sb("kbsel", [1, 4, 32], F32R)
        rind = sb("rind", [P, 32])
        group = sb("group", [P, 4])
        warm = sb("warm", [1, 1])
        kones = sb("kones", [P, 1])
        mhalf = sb("mhalf", [T, B])
        expert = sb("expert", [T, E])
        qbase = sb("qbase", [1, E])
        qbaseB = sb("qbaseB", [1, E], BF16)
        ids = sb("ids", [T, B, TOPK], I32)
        thr = sb("thr", [1, E, NJ])
        upto = sb("upto", [1, E, E])
        tile_no = sb("tile_no", [1, TILES, E])
        tile_row = sb("tile_row", [1, TILES])
        xin = sb("xin", [T, B, D])
        xbo = sb("xbo", [T, B, D])
        cxT = sb("cxT", [P, B, T])
        mraw = sb("mraw", [1, B, T], I32)
        kbias = sb("kbias", [1, B, T], F32R)
        w4 = sb("w4", [P, 4, D])
        bc = sb("bc", [P, 3])
        bo_b = sb("bo_b", [T, D])
        bg_row = sb("bg_row", [1, E])
        ones1 = sb("ones1", [1, T])
        wg_sb = sb("wg_sb", [P, E])
        wf = sb("wf", [P, E, WE])
        zrow = wf[:, E - 1, 0:ZR * XW]
        stats = sb("stats", [T, B, 6])
        mv = sb("mv", [T, B, 2])
        veps = sb("veps", [T, B])
        rstd = sb("rstd", [T, B])
        xn = sb("xn", [P, B, D])
        xnT = sb("xnT", [P, CT])
        kf = sb("kf", [P, CT])
        qf = sb("qf", [P, CT])
        kh = sb("kh", [P, CT], F32R)
        kl = sb("kl", [P, CT], F32R)
        qh = sb("qh", [P, CT], F32R)
        ql = sb("ql", [P, CT], F32R)
        Ks = sb("Ks", [P, B, SLABS, T], F32R)
        Qs = sb("Qs", [P, B, SLABS, T], F32R)
        Kd = sb("Kd", [P, CH, SLABS, 4, T], F32R)
        Qd = sb("Qd", [P, 2, SLABS, 4, T], F32R)
        Va = sb("Va", [P, B, H, 32])
        mx = sb("mx", [T, SLABS, 4])
        mn = sb("mn", [T, SLABS, 4])
        Mp = sb("Mp", [P, 2, SLABS, 4, 32], F32R)
        PT = sb("PT", [P, 2, SLABS, 4, T])
        Tsb = sb("Tsb", [P, 2, SLABS, T])
        rden = sb("rden", [T, H])
        ctxn = sb("ctxn", [T, D])
        coT = sb("coT", [P, T])
        x1 = sb("x1", [T, 2, D])
        stats2 = sb("stats2", [T, 6])
        mv2 = sb("mv2", [T, 2])
        veps2 = sb("veps2", [T, 1])
        rstd2 = sb("rstd2", [T, 1])
        xn2 = sb("xn2", [T, 4, D])
        base = sb("base", [T, B, D])
        xn2T = sb("xn2T", [P, T])
        top = sb("top", [T, 8])
        topi = sb("topi", [T, 8], U32)
        dlt = sb("dlt", [T, TOPK])
        ex = sb("ex", [T, TOPK])
        rd2 = sb("rd2", [T, 1])
        den = sb("den", [T, 1])
        wt = sb("wt", [T, 2, TOPK])
        M = sb("M", [T, TOPK, E])
        Ms = sb("Ms", [T, E], BF16)
        Mprev = sb("Mprev", [T, E], BF16)
        pr = sb("pr", [T, TOPK, E])
        ps = sb("ps", [T, TOPK])
        pos = sb("pos", [T, 2, TOPK], I32)
        xs = sb("xs", [T, 2, TOPK, XW])
        cmp7 = sb("cmp7", [1, E, NJ])
        tiles = sb("tiles", [1, E])
        tpre = sb("tpre", [1, E, E])
        tend = sb("tend", [1, E])
        cmpt = sb("cmpt", [1, TILES, E])
        tcnt = sb("tcnt", [1, TILES])
        cmps = sb("cmps", [1, TILES, E])
        tst = sb("tst", [1, TILES])
        ta = sb("ta", [1, TILES])
        tb = sb("tb", [1, TILES])
        yrow = sb("yrow", [P, 2], I32)
        row_tab = sb("row_tab", [1, TILES], I32)
        exp_tab = sb("exp_tab", [1, TILES], I32)
        room = Va[:].rearrange("p b h r -> p (b h r)")
        sg = room[:, 0:2 * F].rearrange("p (a n) -> p a n", a=2)
        hT = room[:, 2 * F:4 * F].rearrange("p (a n) -> p a n", a=2)
        w1c = room[:, 4 * F:6 * F].rearrange("p (a n) -> p a n", a=2)
        xgT = room[:, 6 * F:6 * F + 2 * P].rearrange("p (a n) -> p a n", a=2)
        ysb = room[:, 6 * F + 2 * P:6 * F + 2 * P + 2 * D].rearrange("p (a n) -> p a n", a=2)
        w3c = xn[:].rearrange("p b d -> p (b d)").rearrange("p (a n) -> p a n", a=2)
        room2 = PT[:].rearrange("p a s c t -> p (a s c t)")
        xg = room2[:, 0:RING * XW].rearrange("p (a n) -> p a n", a=RING)
        yin = room2[0:T, RING * XW:RING * XW + TOPK * B * D].rearrange("p (s b d) -> p s b d", s=TOPK, b=B)
        fin = xin

        x_in, w_in, bc_in, b_in, wf_in, zfill = ([sem("x_in0"), sem("x_in1")], sem("w_in"), sem("bc_in"), sem("b_in"),
                                                 sem("wf_in"), sem("zfill"))
        ctx_in = [sem("ctx_in0"), sem("ctx_in1")]
        scat, y_out, y_in, o_out = [sem("scat0"), sem("scat1")], [sem("y_out0"), sem("y_out1")], [sem("y_in0"), sem("y_in1")], sem("o_out")
        tile_in = [sem(f"tile_in{k}") for k in range(RING)]
        pool_c, dve_c, c_id, z_c, v_c = sem("pool_c"), sem("dve_c"), sem("c_id"), sem("z_c"), sem("v_c")
        names = ("ln_st ln_ag ln_ve ln_rs xn_r prep_ps prep_A prep_V kh_r kl_r qh_r ql_r Kd_r "
                 "s1_ps max_r mh_r ml_r qa_ps qa_r s2_ps exp_r p_r pv_ps t_r tt_ps rd_r cn_r ct_ps "
                 "coT_r wo_ps x1_r l2_st l2_ag l2_ve l2_rs xn2_r x2T_ps x2T_r lg_ps top_r topi_r "
                 "dl_r ex_r rd2_r w_r M_r Ms_r mp_r rk_ps pr_r ps_r pos_r xs_r id_r xbo_r cnt_ps "
                 "tab_s tab_r base_r gT_ps gT_r w1c_r w3c_r a_ps b_ps sg_r h_r y_ps ys_r fin_a fin_r").split()
        S = {n: sem(n) for n in names}

        block = st.enter_context(nc.Block())

        def wait_step(eng, n):
            who, count = taken_out(n)
            eng.wait_ge(S["prep_" + who], count)

        @block.sync
        def _(sp):
            xv = x.rearrange("b t d -> t b d")
            for g in range(2):
                sp.dma_start(xin[:, g * CH:(g + 1) * CH, :], xv[:, g * CH:(g + 1) * CH, :]).then_inc(x_in[g], 16)
                if g == 0:
                    sp.dma_start(w4[:], wqkvo).then_inc(w_in, 16)
            sp.dma_start(cxT[:, CH:B, :], ctxT[:, CH:B, :]).then_inc(ctx_in[1], 16)
            sp.dma_start(bo_b[:], bo.rearrange("(a n) -> a n", a=1).broadcast_to([T, D])).then_inc(b_in, 16)
            sp.dma_start(bg_row[:], bg.rearrange("(a n) -> a n", a=1)).then_inc(b_in, 16)
            sp.dma_start(wg_sb[:], wg).then_inc(b_in, 16)
            sp.wait_ge(z_c, 1)
            zv = queue.rearrange("(p r) c -> p (r c)", p=P)
            per = ROWS // P
            for a in range(0, per, ZR):
                k = min(ZR, per - a)
                sp.dma_start(zv[:, a * XW:(a + k) * XW], zrow[:, 0:k * XW]).then_inc(zfill, 16)
            for e in range(E):
                if e == E - 1:
                    sp.wait_ge(zfill, 16 * NZ)
                sp.dma_start(wf[:, e, :], wffn[:, e, :]).then_inc(wf_in, 16)
            sp.wait_ge(scat[0], 16 * TOPK * B // 2)
            sp.wait_ge(scat[1], 16 * TOPK * B // 2)
            sp.wait_ge(S["tab_r"], 2)
            for t in range(TILES):
                if t >= RING:
                    sp.wait_ge(y_out[t % 2], 16 * ((t - RING) // 2 + 1))
                r = sp.value_load(row_tab[0:1, t:t + 1], min_val=0, max_val=TRASH)
                sp.dma_start(xg[:, t % RING, :], queue[bass.ds(r, SLOT), :]).then_inc(tile_in[t % RING], 16)
            for c in range(2):
                sp.wait_ge(y_out[c], 16 * TILES // 2)
            yv = y_rows[2:2 + TOPK * B * T, :].rearrange("(s b t) d -> t s b d", s=TOPK, b=B)
            for c in range(2):
                bs = slice(c * B // 2, (c + 1) * B // 2)
                for s in range(TOPK):
                    sp.dma_start(yin[:, s, bs, :], yv[:, s, bs, :]).then_inc(y_in[c], 16)
            ov = out.rearrange("b t d -> t b d")
            for c in range(2):
                bs = slice(c * B // 2, (c + 1) * B // 2)
                sp.wait_ge(S["fin_r"], c + 1)
                sp.dma_start(ov[:, bs, :], fin[:, bs, :]).then_inc(o_out, 16)
            sp.wait_ge(o_out, 32)

        @block.gpsimd
        def _(g):
            g.memset(ident[:], 0.0).then_inc(c_id, 1)
            g.memset(mhalf[:], -0.5).then_inc(c_id, 1)
            g.wait_ge(c_id, 1)
            g.affine_select(out=ident[:], in_=ident[:], compare_op=ALU.not_equal, fill=1.0, base=0,
                            pattern=[[-1, P]], channel_multiplier=1).then_inc(c_id, 1)
            g.memset(causal[:], 0.0).then_inc(c_id, 1)
            g.memset(onesB[:], 1.0).then_inc(c_id, 1)
            g.memset(zrow, 0.0).then_inc(z_c, 1)

            def ln1_pow(g0):
                g.wait_ge(S["ln_ve"], g0 + 1)
                bs = slice(g0 * CH, (g0 + 1) * CH)
                g.tensor_tensor(rstd[:, bs], veps[:, bs], mhalf[:, bs], ALU.pow).then_inc(S["ln_rs"], 1)

            g.wait_ge(c_id, 5)
            ln1_pow(0)
            g.affine_select(out=causal[:], in_=causal[:], compare_op=ALU.is_ge, fill=BIG, base=0,
                            pattern=[[-1, T]], channel_multiplier=1).then_inc(pool_c, 1)
            g.affine_select(out=before[:], in_=onesB[:], compare_op=ALU.is_gt, fill=0.0, base=0,
                            pattern=[[1, T]], channel_multiplier=-1).then_inc(pool_c, 1)
            g.iota(qbase[:], pattern=[[PER_E, E]], base=-TRASH, channel_multiplier=0,
                   allow_small_or_imprecise_dtypes=True).then_inc(pool_c, 1)
            g.memset(ones1[:], 1.0).then_inc(pool_c, 1)
            g.memset(Mp[:].bitcast(U32), 0).then_inc(pool_c, 1)
            g.memset(Va[:, :, :, V_ONE:], 0.0).then_inc(v_c, 1)
            ln1_pow(1)
            g.wait_ge(v_c, 1)
            g.memset(Va[:, :, :, V_ONE:V_ONE + 1], 1.0).then_inc(pool_c, 1)
            g.iota(expert[:], pattern=[[1, E]], base=0, channel_multiplier=0,
                   allow_small_or_imprecise_dtypes=True).then_inc(pool_c, 1)
            g.iota(ids[:], pattern=[[T, B], [B * T, TOPK]], base=2, channel_multiplier=1).then_inc(pool_c, 1)
            g.iota(thr[:], pattern=[[0, E], [SLOT, NJ]], base=0, channel_multiplier=0,
                   allow_small_or_imprecise_dtypes=True).then_inc(pool_c, 1)
            g.iota(tile_no[:], pattern=[[1, TILES], [0, E]], base=0, channel_multiplier=0,
                   allow_small_or_imprecise_dtypes=True).then_inc(pool_c, 1)
            g.iota(tile_row[:], pattern=[[SLOT, TILES]], base=0, channel_multiplier=0,
                   allow_small_or_imprecise_dtypes=True).then_inc(pool_c, 1)
            g.memset(upto[:], 1.0).then_inc(v_c, 1)
            g.wait_ge(v_c, 2)
            g.affine_select(out=upto[:], in_=upto[:], compare_op=ALU.is_ge, fill=0.0, base=0,
                            pattern=[[1, E], [-1, E]], channel_multiplier=0).then_inc(pool_c, 1)

            def ln2_pow(b):
                g.wait_ge(S["l2_ve"], b + 1)
                g.tensor_tensor(rstd2[:], veps2[:], mhalf[:, 0:1], ALU.pow).then_inc(S["l2_rs"], 1)

            def keep_causal(b, u):
                g.wait_ge(S["exp_r"], 2 * b + u + 1)
                v = PT[0:T, b % 2, 2 * u:2 * u + 2].rearrange("p s c t -> p (s c) t")
                g.affine_select(out=v, in_=v, compare_op=ALU.is_ge, fill=0.0, base=0,
                                pattern=[[0, HG], [1, T]], channel_multiplier=-1).then_inc(S["p_r"], 1)

            def residual(b):
                g.wait_ge(S["xn2_r"], b + 1)
                g.tensor_tensor(base[:, b, :], x1[:, b % 2, :], xn2[:, b % 4, :], ALU.add).then_inc(S["base_r"], 1)

            def send(b):
                if b >= 2:
                    g.wait_ge(scat[b % 2], 16 * TOPK * (b // 2))
                g.tensor_copy(xs[:, b % 2, :, D:D + 1].bitcast(I32), ids[:, b, :].unsqueeze(2)).then_inc(S["id_r"], 1)
                g.wait_ge(S["id_r"], b + 1)
                g.wait_ge(S["xs_r"], TOPK * (b + 1))
                g.wait_ge(S["pos_r"], b + 1)
                if b == 0:
                    g.wait_ge(zfill, 16 * NZ)
                for s in range(TOPK):
                    g.indirect_dma_start(queue[:, :], bass.IndirectOffsetOnAxis(ap=pos[:, b % 2, s:s + 1], axis=0),
                                         xs[:, b % 2, s, :], None).then_inc(scat[b % 2], 16)

            g.wait_ge(b_in, 48)
            g.wait_ge(x_in[1], 16)
            for i in range(B + 3):
                if 1 <= i <= B:
                    keep_causal(i - 1, 0)
                if 0 <= i - 2 < B:
                    ln2_pow(i - 2)
                if 1 <= i <= B:
                    keep_causal(i - 1, 1)
                if 0 <= i - 3:
                    send(i - 3)
                if i < B:
                    g.tensor_tensor(xbo[:, i, :], xin[:, i, :], bo_b[:], ALU.add).then_inc(S["xbo_r"], 1)
                if 0 <= i - 2 < B:
                    residual(i - 2)

            for t in range(TILES):
                g.wait_ge(S["ys_r"], t + 1)
                if t >= 2:
                    g.wait_ge(y_out[t % 2], 16 * (t // 2))
                g.indirect_dma_start(y_rows[:, :],
                                     bass.IndirectOffsetOnAxis(ap=yrow[:, t % 2:t % 2 + 1], axis=0),
                                     ysb[:, t % 2, :], None).then_inc(y_out[t % 2], 16)

        @block.scalar
        def _(a):
            a.dma_start(cxT[:, 0:CH, :], ctxT[:, 0:CH, :]).then_inc(ctx_in[0], 16)
            a.dma_start(bc[:], bcols).then_inc(bc_in, 16)
            a.dma_start(mraw[:], mask.rearrange("(a b) t -> a b t", a=1)).then_inc(bc_in, 16)
            a.wait_ge(c_id, 3)
            a.activation(warm[:], ident[0:1, 0:1], ACT.Exp)
            a.wait_ge(bc_in, 32)

            def take_out(g0, kind, k=0):
                n = step_no(g0, kind, k)
                a.wait_ge(S["prep_ps"], n + 1)
                src = bank[step_bank(n)][:, 0:CT]
                if kind == "xT":
                    ins = a.activation(xnT[:], src, ACT.Copy)
                elif kind == "K":
                    ins = a.activation(kf[:], src, ACT.Identity, bias=bc[:, 0:1])
                elif kind == "Q":
                    ins = a.activation(qf[:], src, ACT.Identity, bias=bc[:, 1:2])
                else:
                    a.wait_ge(dve_c, 3)
                    dst, ones = (Ks, kones) if kind == "Ks" else (Qs, rind[:, R_KB:R_KB + 1])
                    ins = a.activation(dst[:, g0 * CH:(g0 + 1) * CH, k, :], src.rearrange("p (b t) -> p b t", b=CH),
                                       ACT.Identity, bias=ones[:, 0:1])
                ins.then_inc(S["prep_A"], 1)

            def qaug_evac(b):
                a.wait_ge(S["qa_ps"], b + 1)
                for c in range(4):
                    m = a.activation(Qd[:, b % 2, :, c, :], bank[4][:, 0:SLABS * T].rearrange("p (s t) -> p s t", s=SLABS),
                                     ACT.Copy, scale=group[:, c:c + 1])
                m.then_inc(S["qa_r"], 1)

            def exps(b, u):
                a.wait_ge(S["s2_ps"], 2 * b + u + 1)
                if b >= 2:
                    a.wait_ge(S["pv_ps"], 2 * (b - 2) + u + 1)
                for j in range(2):
                    m = a.activation(PT[0:T, b % 2, 2 * u + j],
                                     bank[2 + j][0:T, 0:4 * T].rearrange("p (c t) -> p c t", c=4), ACT.Exp,
                                     scale=SCALE)
                m.then_inc(S["exp_r"], 1)

            def t_evac(b):
                a.wait_ge(S["pv_ps"], 2 * b + 2)
                a.activation(Tsb[:, b % 2], bank[5][:, 0:SLABS * T].rearrange("p (s t) -> p s t", s=SLABS),
                             ACT.Copy).then_inc(S["t_r"], 1)

            def coT_evac(b):
                a.wait_ge(S["ct_ps"], b + 1)
                a.activation(coT[:], bank[7][:, 0:T], ACT.Identity, bias=bc[:, 2:3]).then_inc(S["coT_r"], 1)

            def route(b):
                a.wait_ge(S["dl_r"], b + 1)
                a.activation(ex[:], dlt[:], ACT.Exp, accum_out=den[:]).then_inc(S["ex_r"], 1)

            def scale_rows(b):
                a.wait_ge(S["w_r"], b + 1)
                if b >= 2:
                    a.wait_ge(scat[b % 2], 16 * TOPK * (b // 2))
                for s in range(TOPK):
                    a.activation(xs[:, b % 2, s, 0:D], xn2[:, b % 4, :], ACT.Copy,
                                 scale=wt[:, b % 2, s:s + 1]).then_inc(S["xs_r"], 1)

            for kind, k, eng in STEPS:
                if eng == "A":
                    take_out(0, kind, k)
            for i in range(B + 3):
                now, scored, tail, placing = i < B, 1 <= i <= B, 0 <= i - 2 < B, 0 <= i - 3
                if tail:
                    coT_evac(i - 2)
                if scored:
                    exps(i - 1, 0)
                if placing:
                    scale_rows(i - 3)
                if scored:
                    exps(i - 1, 1)
                for kind, k, eng in EARLY.get(i, ()):
                    if eng == "A":
                        take_out(1, kind, k)
                if now:
                    qaug_evac(i)
                for kind, k, eng in LATE.get(i, ()):
                    if eng == "A":
                        take_out(1, kind, k)
                if scored:
                    t_evac(i - 1)
                if tail:
                    route(i - 2)

            wrow = wf[:].rearrange("p e n -> p (e n)")

            def fetch_w1(t):
                e = a.value_load(exp_tab[0:1, t:t + 1], min_val=0, max_val=(E - 1) * WE)
                if t >= 2:
                    a.wait_ge(S["a_ps"], t - 1)
                a.activation(w1c[:, t % 2, :], wrow[:, bass.ds(e, F)], ACT.Copy).then_inc(S["w1c_r"], 1)

            def silu(t):
                a.wait_ge(S["a_ps"], t + 1)
                if t >= 2:
                    a.wait_ge(S["h_r"], t - 1)
                a.activation(sg[:, t % 2, :], bank[1 + t % 2][:], ACT.Silu).then_inc(S["sg_r"], 1)

            a.wait_ge(wf_in, 16 * E)
            a.wait_ge(S["tab_r"], 2)
            fetch_w1(0)
            fetch_w1(1)
            for t in range(TILES):
                silu(t)
                if t + 2 < TILES:
                    fetch_w1(t + 2)

        @block.tensor
        def _(pe):
            pe.wait_ge(c_id, 3)

            def prepare(g0, kind, k=0):
                n = step_no(g0, kind, k)
                if step_before(n) is not None:
                    wait_step(pe, step_before(n))
                o = bank[step_bank(n)]
                flat = "p c j d -> p (c j d)"
                if kind == "xT":
                    pe.wait_ge(S["xn_r"], g0 + 1)
                    for b in range(CH):
                        m = pe.transpose(o[:, b * T:(b + 1) * T], xn[0:T, g0 * CH + b, :], ident[0:T, 0:T])
                elif kind == "K":
                    pe.wait_ge(ctx_in[g0], 16)
                    pe.wait_ge(w_in, 16)
                    m = pe.matmul(o[:, 0:CT], w4[:, 1, :], cxT[:, g0 * CH:(g0 + 1) * CH, :].rearrange("p b t -> p (b t)"),
                                  start=True, stop=True)
                elif kind == "Q":
                    wait_step(pe, step_no(g0, "xT"))
                    m = pe.matmul(o[:, 0:CT], w4[:, 0, :], xnT[:], start=True, stop=True)
                elif kind == "V":
                    for b in range(2):
                        m = pe.matmul(o[0:T, b * D:(b + 1) * D], cxT[:, g0 * CH + 2 * k + b, :], w4[:, 2, :],
                                      start=True, stop=True)
                elif kind == "Ks":
                    pe.wait_ge(S["kl_r"], g0 + 1)
                    pe.wait_ge(dve_c, 3)
                    pe.matmul(o[:, 0:CT], selKH[:, k].rearrange(flat), kh[:], start=True, stop=False)
                    pe.matmul(o[:, 0:CT], selKL[:, k].rearrange(flat), kl[:], start=False, stop=False)
                    m = pe.matmul(o[:, 0:CT], kbsel[:].rearrange("p c r -> p (c r)"),
                                  kbias[:, g0 * CH:(g0 + 1) * CH, :].rearrange("p b t -> p (b t)"),
                                  start=False, stop=True)
                else:
                    pe.wait_ge(S["ql_r"], g0 + 1)
                    pe.matmul(o[:, 0:CT], selQH[:, k].rearrange(flat), qh[:], start=True, stop=False)
                    m = pe.matmul(o[:, 0:CT], selQL[:, k].rearrange(flat), ql[:], start=False, stop=True)
                m.then_inc(S["prep_ps"], 1)

            def s1(b, s):
                n = SLABS * b + s
                if n >= 2:
                    pe.wait_ge(S["max_r"], n - 1)
                o = bank[s % 2][0:T, 0:4 * T].rearrange("p (c t) -> p c t", c=4)
                pe.matmul(o, identB[:, 0:T], causal[:].unsqueeze(1).broadcast_to([P, 4, T]), start=True, stop=False)
                pe.matmul(o, Qs[:, b, s, :], Kd[:, b % CH, s], start=False, stop=True).then_inc(S["s1_ps"], 1)

            def place_queries(b):
                if b >= 1:
                    pe.wait_ge(S["qa_r"], b)
                pe.matmul(bank[4][:, 0:SLABS * T], identR[:], Qs[:, b].rearrange("p s t -> p (s t)"), start=True,
                          stop=False, skip_group_check=True)

            def place_max(b):
                pe.wait_ge(S["ml_r"], b + 1)
                for s in range(SLABS):
                    m = pe.matmul(bank[4][:, s * T:(s + 1) * T], Mp[:, b % 2, s].rearrange("p c r -> p (c r)"),
                                  identR[:, 0:T], start=False, stop=True, skip_group_check=True)
                m.then_inc(S["qa_ps"], 1)

            def s2(b, u):
                pe.wait_ge(S["qa_r"], b + 1)
                if 2 * b + u >= 1:
                    pe.wait_ge(S["exp_r"], 2 * b + u)
                for j in range(2):
                    s = 2 * u + j
                    m = pe.matmul(bank[2 + j][0:T, 0:4 * T], Ks[:, b, s, :],
                                  Qd[:, b % 2, s].rearrange("p c t -> p (c t)"), start=True, stop=True)
                m.then_inc(S["s2_ps"], 1)

            def pv(b, u):
                if b >= 1 and u == 0:
                    pe.wait_ge(S["t_r"], b)
                if u == 0 and b % CH == 0:
                    wait_step(pe, step_no(b // CH, "V", 1))
                    pe.wait_ge(pool_c, 6)
                if u == 0 and b == 0:
                    wait_step(pe, step_no(1, "Ks", SLABS - 1))
                pe.wait_ge(S["p_r"], 2 * b + u + 1)
                for s in (2 * u, 2 * u + 1):
                    for c in range(4):
                        m = pe.matmul(bank[5][32 * c:32 * c + 32, s * T:(s + 1) * T], Va[0:T, b, 4 * s + c, :],
                                      PT[0:T, b % 2, s, c, :], start=True, stop=True)
                m.then_inc(S["pv_ps"], 1)

            def t_turn(b):
                pe.wait_ge(S["t_r"], b + 1)
                if b >= 1:
                    pe.wait_ge(S["x1_r"], b)
                else:
                    wait_step(pe, step_no(1, "Qs", 3))
                for s in range(SLABS):
                    m = pe.transpose(bank[7][0:T, s * P:(s + 1) * P], Tsb[:, b % 2, s, :], ident[:])
                m.then_inc(S["tt_ps"], 1)

            def ctx_turn(b):
                pe.wait_ge(S["cn_r"], b + 1)
                pe.transpose(bank[7][:, 0:T], ctxn[:], ident[0:T, 0:T]).then_inc(S["ct_ps"], 1)

            def wo(b):
                pe.wait_ge(S["coT_r"], b + 1)
                pe.matmul(bank[7][0:T, P:P + D], coT[:], w4[:, 3, :], start=True, stop=True).then_inc(S["wo_ps"], 1)

            def xn2_turn(b):
                pe.wait_ge(S["xn2_r"], b + 1)
                if b == 0:
                    wait_step(pe, 2 * NSTEP - 1)
                    pe.wait_ge(b_in, 48)
                else:
                    pe.wait_ge(S["pr_r"], b)
                pe.transpose(bank[6][:, 0:T], xn2[:, b % 4, :], ident[0:T, 0:T]).then_inc(S["x2T_ps"], 1)

            def logits(b):
                pe.wait_ge(S["x2T_r"], b + 1)
                pe.matmul(bank[6][0:T, 0:E], xn2T[:], wg_sb[:], start=True, stop=False)
                pe.matmul(bank[6][0:T, 0:E], ones1[:], bg_row[:], start=False, stop=True).then_inc(S["lg_ps"], 1)

            def rank(b):
                pe.wait_ge(S["Ms_r"], b + 1)
                if b >= 1:
                    pe.wait_ge(S["mp_r"], b)
                if b == 0:
                    pe.wait_ge(dve_c, 7)
                pe.matmul(bank[6][0:T, 0:E], onesB[0:1, :], qbaseB[:], start=True, stop=False)
                pe.matmul(bank[6][0:T, 0:E], before[:], Ms[:], start=False, stop=False)
                pe.matmul(bank[6][0:T, 0:E], onesB[:], Mprev[:], start=False, stop=True).then_inc(S["rk_ps"], 1)

            for kind, k, _ in STEPS:
                prepare(0, kind, k)
            pe.wait_ge(pool_c, 1)
            for i in range(B + 3):
                now, scored, tail, placing = i < B, 1 <= i <= B, 0 <= i - 2 < B, 0 <= i - 3
                if i in (0, CH):
                    g0 = i // CH
                    wait_step(pe, step_no(g0, "Qs", 2))
                    wait_step(pe, step_no(g0, "Qs", 3))
                if now:
                    pe.wait_ge(S["Kd_r"], i + 1)
                    s1(i, 0)
                    s1(i, 1)
                if placing:
                    rank(i - 3)
                if tail:
                    ctx_turn(i - 2)
                if scored:
                    s2(i - 1, 0)
                if now:
                    s1(i, 2)
                if tail:
                    wo(i - 2)
                if now:
                    s1(i, 3)
                if scored:
                    s2(i - 1, 1)
                for kind, k, _ in EARLY.get(i, ()):
                    prepare(1, kind, k)
                if now:
                    place_queries(i)
                if scored:
                    pv(i - 1, 0)
                if now:
                    place_max(i)
                for kind, k, _ in LATE.get(i, ()):
                    prepare(1, kind, k)
                if tail:
                    xn2_turn(i - 2)
                if scored:
                    pv(i - 1, 1)
                if tail:
                    logits(i - 2)
                if scored:
                    t_turn(i - 1)
            pe.wait_ge(S["pr_r"], B)
            pe.wait_ge(S["mp_r"], B)
            pe.matmul(bank[6][0:T, 0:E], onesB[:], Mprev[:], start=True, stop=True).then_inc(S["cnt_ps"], 1)

            def x_turn(t):
                pe.wait_ge(tile_in[t % RING], 16 * (t // RING + 1))
                if t >= 1:
                    pe.wait_ge(S["gT_r"], t)
                pe.transpose(bank[0][:, 0:P], xg[:, t % RING, 0:D], ident[:]).then_inc(S["gT_ps"], 1)

            def which(t):
                return pe.value_load(exp_tab[0:1, t:t + 1], min_val=0, max_val=(E - 1) * WE)

            def up(t):
                pe.wait_ge(S["gT_r"], t + 1)
                for w, done, fetched, o, free in ((w1c, "a_ps", "w1c_r", bank[1 + t % 2], "sg_r"),
                                                  (w3c, "b_ps", "w3c_r", bank[3 + 2 * (t % 2)], "h_r")):
                    pe.wait_ge(S[fetched], t + 1)
                    if t >= 2:
                        pe.wait_ge(S[free], t - 1)
                    for c in range(FC):
                        m = pe.matmul(o[:, c * P:(c + 1) * P], w[:, t % 2, c * P:(c + 1) * P], xgT[:, t % 2, :],
                                      start=True, stop=True)
                    m.then_inc(S[done], 1)

            def down(t, e):
                wrow = wf[:].rearrange("p e n -> p (e n)")
                pe.wait_ge(S["h_r"], t + 1)
                if t >= 2:
                    pe.wait_ge(S["ys_r"], t - 1)
                for c in range(FC):
                    m = pe.matmul(bank[4 + 3 * (t % 2)][:, 0:D], hT[:, t % 2, c * P:(c + 1) * P],
                                  wrow[:, bass.ds(e + 2 * F + c * D, D)], start=(c == 0), stop=(c == FC - 1))
                m.then_inc(S["y_ps"], 1)

            pe.wait_ge(wf_in, 16 * E)
            pe.wait_ge(S["tab_r"], 2)
            x_turn(0)
            ex_of = {0: which(0)}
            up(0)
            x_turn(1)
            for t in range(TILES):
                if t + 1 < TILES:
                    up(t + 1)
                    ex_of[t + 1] = which(t + 1)
                if t + 2 < TILES:
                    x_turn(t + 2)
                down(t, ex_of.pop(t))

        @block.vector
        def _(v):
            def ln1_stats(g0):
                v.wait_ge(x_in[g0], 16)
                for b in range(g0 * CH, (g0 + 1) * CH):
                    m = v.bn_stats(stats[:, b, :], xin[:, b, :])
                m.then_inc(S["ln_st"], 1)
                v.wait_ge(S["ln_st"], g0 + 1)
                for b in range(g0 * CH, (g0 + 1) * CH):
                    m = v.bn_aggr(mv[:, b, :], stats[:, b, :])
                m.then_inc(S["ln_ag"], 1)
                v.wait_ge(S["ln_ag"], g0 + 1)
                v.tensor_scalar(veps[:, g0 * CH:(g0 + 1) * CH], mv[:, g0 * CH:(g0 + 1) * CH, 1], EPS, None, ALU.add)\
                    .then_inc(S["ln_ve"], 1)

            def ln1_apply(g0):
                v.wait_ge(S["ln_rs"], g0 + 1)
                for b in range(g0 * CH, (g0 + 1) * CH):
                    m = v.tensor_scalar(xn[0:T, b, :], xin[:, b, :], mv[:, b, 0:1], rstd[:, b:b + 1], ALU.subtract, ALU.mult)
                m.then_inc(S["xn_r"], 1)

            def take_out(g0, kind, k=0):
                n = step_no(g0, kind, k)
                v.wait_ge(S["prep_ps"], n + 1)
                o = bank[step_bank(n)]
                if kind == "V":
                    b = g0 * CH + 2 * k
                    ins = v.tensor_copy(Va[0:T, b:b + 2, :, 0:DK],
                                        o[0:T, 0:2 * D].rearrange("p (b h d) -> p b h d", b=2, h=H))
                else:
                    ins = v.tensor_scalar(Qs[:, g0 * CH:(g0 + 1) * CH, k, :],
                                          o[:, 0:CT].rearrange("p (b t) -> p b t", b=CH), rind[:, R_KB:R_KB + 1], None,
                                          ALU.add)
                ins.then_inc(S["prep_V"], 1)

            def split_high(g0, full, high, kind, done):
                wait_step(v, step_no(g0, kind))
                v.tensor_copy(high[:], full[:]).then_inc(done, 1)

            def spread(g0, b):
                if b == g0 * CH:
                    wait_step(v, step_no(g0, "Ks", SLABS - 1))
                    v.wait_ge(dve_c, 4)
                if b >= CH:
                    v.wait_ge(S["s1_ps"], SLABS * (b - CH + 1))
                for c in range(4):
                    m = v.tensor_scalar(Kd[:, b % CH, :, c, :], Ks[:, b].bitcast(F32), group[:, c:c + 1], None, ALU.mult)
                m.then_inc(S["Kd_r"], 1)

            def split_low(g0, full, high, low, ready, done):
                v.wait_ge(ready, g0 + 1)
                v.tensor_tensor(low[:], full[:], high[:].bitcast(F32), ALU.subtract).then_inc(done, 1)

            v.memset(selKH[:].bitcast(U32), 0)
            v.memset(selKL[:].bitcast(U32), 0)
            v.memset(selQH[:].bitcast(U32), 0)
            v.memset(selQL[:].bitcast(U32), 0)
            v.memset(kbsel[:].bitcast(U32), 0).then_inc(dve_c, 1)
            ln1_stats(0)
            v.wait_ge(c_id, 3)
            v.wait_ge(dve_c, 1)
            v.tensor_scalar(kbsel[:, :, R_KB:R_KB + 1], kbsel[:, :, R_KB:R_KB + 1].bitcast(F32), 1.0, None, ALU.add)
            iv = ident[:].rearrange("p (s c d) -> p s c d", s=SLABS, c=4)
            for j in (0, 2):
                v.tensor_copy(selKH[:, :, :, j, :], iv)
            v.tensor_copy(selKL[:, :, :, 1, :], iv)
            v.tensor_reduce(rind[:], ident[:].rearrange("p (c r) -> p r c", c=4), AX.X, ALU.add).then_inc(dve_c, 1)
            ln1_apply(0)
            v.wait_ge(dve_c, 2)
            v.tensor_tensor(kones[:], rind[:, R_MH:R_MH + 1], rind[:, R_ML:R_ML + 1], ALU.add)
            v.wait_ge(bc_in, 32)
            v.tensor_scalar(kbias[:], mraw[:], 0.0, BIG, ALU.is_equal, ALU.mult).then_inc(dve_c, 1)
            split_high(0, kf, kh, "K", S["kh_r"])
            split_low(0, kf, kh, kl, S["kh_r"], S["kl_r"])
            for j in (0, 1):
                v.tensor_copy(selQH[:, :, :, j, :], iv)
            v.tensor_copy(selQL[:, :, :, 2, :], iv)
            v.tensor_reduce(group[:], ident[:].rearrange("p (c r) -> p c r", c=4), AX.X, ALU.add).then_inc(dve_c, 1)
            split_high(0, qf, qh, "Q", S["qh_r"])
            split_low(0, qf, qh, ql, S["qh_r"], S["ql_r"])
            v.tensor_copy(identR[:], ident[:])
            v.tensor_copy(identB[:], ident[:]).then_inc(dve_c, 1)
            v.memset(dlt[:], 0.0)
            v.memset(Mprev[:], 0.0).then_inc(dve_c, 1)
            spread(0, 0)
            take_out(0, "Qs", 1)
            take_out(0, "Qs", 3)
            take_out(0, "V", 0)
            take_out(0, "V", 1)
            ln1_stats(1)

            def maxima(b, s):
                v.wait_ge(S["s1_ps"], SLABS * b + s + 1)
                v.tensor_reduce(mx[:, s], bank[s % 2][0:T, 0:4 * T].rearrange("p (c t) -> p c t", c=4),
                                AX.X, ALU.max).then_inc(S["max_r"], 1)

            def negate_max(b):
                v.wait_ge(S["max_r"], 4 * b + 4)
                mp = Mp[0:T, b % 2]
                if b == 0:
                    v.wait_ge(pool_c, 5)
                if b >= 2:
                    v.wait_ge(S["qa_ps"], b - 1)
                v.tensor_scalar(mn[:], mx[:], -1.0, CLAMP, ALU.mult, ALU.min)
                v.tensor_scalar(mp[:, :, :, R_MH], mx[:], -1.0, CLAMP, ALU.mult, ALU.min).then_inc(S["mh_r"], 1)

            def negated_low(b):
                v.wait_ge(S["mh_r"], b + 1)
                mp = Mp[0:T, b % 2]
                v.tensor_tensor(mp[:, :, :, R_ML], mn[:], mp[:, :, :, R_MH].bitcast(F32), ALU.subtract)\
                    .then_inc(S["ml_r"], 1)

            def invert_sums(b):
                v.wait_ge(S["tt_ps"], b + 1)
                v.reciprocal(rden[:], bank[7][0:T, :].rearrange("p (h r) -> p h r", h=H)[:, :, V_ONE])\
                    .then_inc(S["rd_r"], 1)

            def norm(b):
                v.wait_ge(S["rd_r"], b + 1)
                o = bank[7][0:T, :].rearrange("p (h r) -> p h r", h=H)
                v.tensor_tensor(ctxn[:].rearrange("p (h d) -> p h d", h=H), o[:, :, 0:DK],
                                rden[:].unsqueeze(2).broadcast_to([T, H, DK]), ALU.mult).then_inc(S["cn_r"], 1)

            def add_x(b):
                v.wait_ge(S["wo_ps"], b + 1)
                v.wait_ge(S["xbo_r"], b + 1)
                if b >= 2:
                    v.wait_ge(S["base_r"], b - 1)
                v.tensor_tensor(x1[:, b % 2, :], bank[7][0:T, P:P + D], xbo[:, b, :], ALU.add).then_inc(S["x1_r"], 1)

            def ln2_stats(b):
                v.wait_ge(S["x1_r"], b + 1)
                v.bn_stats(stats2[:], x1[:, b % 2, :]).then_inc(S["l2_st"], 1)

            def ln2_mean(b):
                v.wait_ge(S["l2_st"], b + 1)
                v.bn_aggr(mv2[:], stats2[:]).then_inc(S["l2_ag"], 1)

            def ln2_guard(b):
                v.wait_ge(S["l2_ag"], b + 1)
                v.tensor_scalar(veps2[:], mv2[:, 1:2], EPS, None, ALU.add).then_inc(S["l2_ve"], 1)

            def ln2_apply(b):
                v.wait_ge(S["l2_rs"], b + 1)
                if b >= 4:
                    v.wait_ge(S["xs_r"], TOPK * (b - 3))
                v.tensor_scalar(xn2[:, b % 4, :], x1[:, b % 2, :], mv2[:, 0:1], rstd2[:], ALU.subtract, ALU.mult)\
                    .then_inc(S["xn2_r"], 1)

            def xn2T_evac(b):
                v.wait_ge(S["x2T_ps"], b + 1)
                v.tensor_copy(xn2T[:], bank[6][:, 0:T]).then_inc(S["x2T_r"], 1)

            def top_logits(b):
                v.wait_ge(S["lg_ps"], b + 1)
                v.max(top[:], bank[6][0:T, 0:E]).then_inc(S["top_r"], 1)

            def top_experts(b):
                v.wait_ge(S["top_r"], b + 1)
                v.max_index(topi[:], top[:], bank[6][0:T, 0:E]).then_inc(S["topi_r"], 1)
                v.tensor_tensor(dlt[:, 1:2], top[:, 1:2], top[:, 0:1], ALU.subtract).then_inc(S["dl_r"], 1)

            def one_hot(b):
                v.wait_ge(S["topi_r"], b + 1)
                v.tensor_tensor(M[:], expert[:].unsqueeze(1).broadcast_to([T, TOPK, E]),
                                topi[:, 0:TOPK].unsqueeze(2).broadcast_to([T, TOPK, E]), ALU.is_equal)\
                    .then_inc(S["M_r"], 1)
                if b >= 1:
                    v.wait_ge(S["rk_ps"], b)
                    v.tensor_tensor(Mprev[:], Mprev[:], Ms[:], ALU.add).then_inc(S["mp_r"], 1)

            def both_experts(b):
                v.wait_ge(S["M_r"], b + 1)
                if b >= 1:
                    v.wait_ge(S["mp_r"], b)
                v.tensor_tensor(Ms[:], M[:, 0, :], M[:, 1, :], ALU.add).then_inc(S["Ms_r"], 1)

            def invert_den(b):
                v.wait_ge(S["ex_r"], b + 1)
                v.reciprocal(rd2[:], den[:]).then_inc(S["rd2_r"], 1)

            def weigh(b):
                v.wait_ge(S["rd2_r"], b + 1)
                if b >= 2:
                    v.wait_ge(S["xs_r"], TOPK * (b - 1))
                v.tensor_scalar(wt[:, b % 2, :], ex[:], rd2[:], None, ALU.mult).then_inc(S["w_r"], 1)

            def pick_rank(b):
                v.wait_ge(S["rk_ps"], b + 1)
                v.tensor_tensor(pr[:], M[:], bank[6][0:T, 0:E].unsqueeze(1).broadcast_to([T, TOPK, E]), ALU.mult)\
                    .then_inc(S["pr_r"], 1)

            def sum_rank(b):
                v.wait_ge(S["pr_r"], b + 1)
                v.tensor_reduce(ps[:], pr[:], AX.X, ALU.add).then_inc(S["ps_r"], 1)

            def place(b):
                v.wait_ge(S["ps_r"], b + 1)
                if b >= 2:
                    v.wait_ge(scat[b % 2], 16 * TOPK * (b // 2))
                v.tensor_scalar(pos[:, b % 2, :], ps[:], float(TRASH), None, ALU.add).then_inc(S["pos_r"], 1)

            for i in range(B + 3):
                now, tail, placing = i < B, 0 <= i - 2 < B, 0 <= i - 3
                if tail:
                    invert_sums(i - 2)
                if placing:
                    invert_den(i - 3)
                if tail:
                    norm(i - 2)
                if placing:
                    weigh(i - 3)
                if now:
                    maxima(i, 0)
                if placing:
                    pick_rank(i - 3)
                if now:
                    maxima(i, 1)
                if placing:
                    sum_rank(i - 3)
                if tail:
                    add_x(i - 2)
                if placing:
                    place(i - 3)
                if i == 0:
                    ln1_apply(1)
                if now:
                    maxima(i, 2)
                if tail:
                    ln2_stats(i - 2)
                if now:
                    maxima(i, 3)
                if tail:
                    ln2_mean(i - 2)
                if i == 1:
                    take_out(1, "Qs", 1)
                if now:
                    negate_max(i)
                if tail:
                    ln2_guard(i - 2)
                if now:
                    negated_low(i)
                if i == 0:
                    split_high(1, kf, kh, "K", S["kh_r"])
                    split_low(1, kf, kh, kl, S["kh_r"], S["kl_r"])
                    split_high(1, qf, qh, "Q", S["qh_r"])
                    split_low(1, qf, qh, ql, S["qh_r"], S["ql_r"])
                    spread(0, 1)
                if i == 1:
                    v.wait_ge(pool_c, 12)
                    v.wait_ge(dve_c, 6)
                    v.tensor_copy(qbaseB[:], qbase[:]).then_inc(dve_c, 1)
                if i == 1:
                    take_out(1, "Qs", 3)
                if i == 2:
                    take_out(1, "V", 0)
                    take_out(1, "V", 1)
                if tail:
                    ln2_apply(i - 2)
                    xn2T_evac(i - 2)
                    top_logits(i - 2)
                    top_experts(i - 2)
                    one_hot(i - 2)
                    both_experts(i - 2)
                for b in SPREADS.get(i, ()):
                    spread(b // CH, b)
            v.tensor_tensor(Mprev[:], Mprev[:], Ms[:], ALU.add).then_inc(S["mp_r"], 1)
            tab = [0]

            def link(ins):
                tab[0] += 1
                ins.then_inc(S["tab_s"], 1)
                v.wait_ge(S["tab_s"], tab[0])

            v.wait_ge(S["cnt_ps"], 1)
            link(v.tensor_tensor(cmp7[:], bank[6][0:1, 0:E].unsqueeze(2).broadcast_to([1, E, NJ]), thr[:], ALU.is_gt))
            link(v.tensor_reduce(tiles[:], cmp7[:], AX.X, ALU.add))
            link(v.tensor_tensor(tpre[:], tiles[:].unsqueeze(1).broadcast_to([1, E, E]), upto[:], ALU.mult))
            link(v.tensor_reduce(tend[:], tpre[:], AX.X, ALU.add))
            link(v.tensor_tensor(cmpt[:], tend[:].unsqueeze(1).broadcast_to([1, TILES, E]), tile_no[:], ALU.is_le))
            link(v.tensor_reduce(tcnt[:], cmpt[:], AX.X, ALU.add))
            link(v.tensor_scalar(exp_tab[:], tcnt[:], float(E - 1), float(WE), ALU.min, ALU.mult))
            link(v.tensor_tensor(cmps[:], tiles[:].unsqueeze(1).broadcast_to([1, TILES, E]), cmpt[:], ALU.mult))
            link(v.tensor_reduce(tst[:], cmps[:], AX.X, ALU.add))
            link(v.scalar_tensor_tensor(ta[:], tst[:], -float(SLOT), tile_row[:], ALU.mult, ALU.add))
            link(v.scalar_tensor_tensor(tb[:], tcnt[:], float(PER_E), ta[:], ALU.mult, ALU.add))
            v.tensor_scalar(row_tab[:], tb[:], float(TRASH), None, ALU.min).then_inc(S["tab_r"], 2)

            def gT_evac(t):
                v.wait_ge(S["gT_ps"], t + 1)
                if t >= 2:
                    v.wait_ge(S["b_ps"], t - 1)
                v.tensor_copy(xgT[:, t % 2, :], bank[0][:, 0:P]).then_inc(S["gT_r"], 1)

            wrow = wf[:].rearrange("p e n -> p (e n)")

            def fetch_w3(t):
                e = v.value_load(exp_tab[0:1, t:t + 1], min_val=0, max_val=(E - 1) * WE)
                if t >= 2:
                    v.wait_ge(S["b_ps"], t - 1)
                v.tensor_copy(w3c[:, t % 2, :], wrow[:, bass.ds(e + F, F)]).then_inc(S["w3c_r"], 1)

            def gate(t):
                v.wait_ge(S["sg_r"], t + 1)
                v.wait_ge(S["b_ps"], t + 1)
                if t >= 2:
                    v.wait_ge(S["y_ps"], t - 1)
                v.tensor_tensor(hT[:, t % 2, :], sg[:, t % 2, :], bank[3 + 2 * (t % 2)][:], ALU.mult).then_inc(S["h_r"], 1)

            def y_evac(t):
                v.wait_ge(S["y_ps"], t + 1)
                if t >= 2:
                    v.wait_ge(y_out[t % 2], 16 * (t // 2))
                v.tensor_scalar(yrow[:, t % 2:t % 2 + 1], xg[:, t % RING, D:D + 1].bitcast(I32), float(t % 2), None,
                                ALU.max)
                v.tensor_copy(ysb[:, t % 2, :], bank[4 + 3 * (t % 2)][:, 0:D]).then_inc(S["ys_r"], 1)

            v.wait_ge(wf_in, 16 * E)
            v.wait_ge(S["tab_r"], 2)
            fetch_w3(0)
            fetch_w3(1)
            gT_evac(0)
            gT_evac(1)
            for t in range(TILES):
                gate(t)
                if t + 2 < TILES:
                    fetch_w3(t + 2)
                if t >= 1:
                    y_evac(t - 1)
                if t + 2 < TILES:
                    gT_evac(t + 2)
            y_evac(TILES - 1)
            for c in range(2):
                bs = slice(c * B // 2, (c + 1) * B // 2)
                v.wait_ge(y_in[c], 16 * TOPK)
                v.wait_ge(S["base_r"], B)
                v.tensor_tensor(fin[:, bs, :], yin[:, 0, bs, :], yin[:, 1, bs, :], ALU.add).then_inc(S["fin_a"], 1)
                v.wait_ge(S["fin_a"], c + 1)
                v.tensor_tensor(fin[:, bs, :], fin[:, bs, :], base[:, bs, :], ALU.add).then_inc(S["fin_r"], 1)


def kernel(**inputs):
    import numpy as np
    import concourse.bacc as bacc
    from concourse.bass_utils import run_bass_kernel_spmd

    i = {k: np.asarray(v) for k, v in inputs.items()}
    w = [i["L0_xattn_" + n] for n in ("Wq", "Wk", "Wv", "Wo")]
    e13 = np.stack([i["L0_ffn_W1"], i["L0_ffn_W3"]], axis=2)
    e2 = i["L0_ffn_W2"].reshape(E, FC, P, D).transpose(2, 0, 1, 3)
    arrays = {
        "x": i["x"],
        "ctxT": i["ctx_1024"][:, :T, :].transpose(2, 0, 1),
        "mask": i["mask_BxS2_if1"][:, :T],
        "wqkvo": np.stack([a.T for a in w], axis=1),
        "bcols": np.stack([i["L0_xattn_bk"], i["L0_xattn_bq"], i["L0_xattn_bv"]], axis=1),
        "bo": i["L0_xattn_bo"],
        "wg": i["L0_ffn_Wg"],
        "bg": i["L0_ffn_bg"],
        "wffn": np.concatenate([e13.transpose(1, 0, 2, 3).reshape(P, E, 2 * F), e2.reshape(P, E, FC * D)], axis=2),
    }
    arrays = {k: np.ascontiguousarray(a) for k, a in arrays.items()}
    nc = bacc.Bacc("TRN2", target_bir_lowering=False, num_devices=1)
    args = [nc.dram_tensor(k, a.shape, mybir.dt.from_np(a.dtype), kind="ExternalInput").ap() for k, a in arrays.items()]
    args.append(nc.dram_tensor("out", (B, T, D), F32, kind="ExternalOutput").ap())
    bass_xattn_moe(nc, *args)
    r = run_bass_kernel_spmd(nc, [arrays], core_ids=[0])
    return r.results[0]["out"]
```

```python
from contextlib import ExitStack

import concourse.bass as bass
from concourse import mybir
from concourse.alu_op_type import AluOpType as ALU

ACT = mybir.ActivationFunctionType
AX = mybir.AxisListType
F32 = mybir.dt.float32
F32R = mybir.dt.float32r
BF16 = mybir.dt.bfloat16
I32 = mybir.dt.int32
U32 = mybir.dt.uint32

P = 128
B = 8
T = 100
D = 128
H = 16
DK = D // H
SLABS = H // 4
HG = H // 2
E = 8
F = 512
FC = F // P
WE = 2 * F + FC * D
TOPK = 2
EPS = 1e-5
SCALE = float(DK) ** -0.5
BIG = -1e30
CLAMP = 1e29

R_MH, R_ML, R_KB = 24, 25, 26
V_ONE = DK

SLOT = P
PER_E = (B * T + SLOT - 1) // SLOT * SLOT
TRASH = E * PER_E
ROWS = TRASH + SLOT
TILES = (B * T * TOPK + E * (SLOT - 1)) // SLOT
NJ = PER_E // SLOT
RING = 4
TURNS = TILES // RING
assert TILES % RING == 0 and TURNS > 2

CH = B // 2
CT = CH * T
PROJ = [("K", 0, "A"), ("xT", 0, "A"), ("Q", 0, "A")]
SLAB = [("Ks", s, "A") for s in range(SLABS)] + [("Qs", s, "V" if s % 2 else "A") for s in range(SLABS)]
VALUES = [("V", 0, "V"), ("V", 1, "V")]
NSTEP = len(PROJ + SLAB + VALUES)
LATER = PROJ[0:2] + VALUES + PROJ[2:3] + SLAB
STEPS = PROJ + SLAB + VALUES + LATER
BANKS = [n % 4 for n in range(NSTEP - 2)] + [5, 7] + [5, 6, 7, 5] + [6, 7, 6, 7] + [6, 6, 6, 6, 6]


def step_before(n):
    had = [m for m in range(n) if BANKS[m] == BANKS[n]]
    return had[-1] if had else None


def taken_out(n):
    eng = STEPS[n][2]
    return eng, sum(STEPS[m][2] == eng for m in range(n + 1))


def step_no(g, kind, k=0):
    return g * NSTEP + [(a, b) for a, b, _ in STEPS[g * NSTEP:(g + 1) * NSTEP]].index((kind, k))


def beside(i, place):
    count = {(0, 1): 1, (0, 2): 3, (1, 0): 1, (1, 1): 1, (1, 2): 2, (2, 0): 1, (2, 1): 1, (2, 2): 2, (3, 0): 1}
    start = sum(c for at, c in count.items() if at < (i, place))
    return LATER[start:start + count.get((i, place), 0)]


SPREADS_V = {-1: (0, 1), 1: (2,), 2: (3,), 3: (5,), 5: (7,)}
SPREADS_A = {2: (4,), 4: (6,)}


def spread_by(b):
    for who, table in (("V", SPREADS_V), ("A", SPREADS_A)):
        mine = [x for i in sorted(table) for x in table[i]]
        if b in mine:
            return who, mine.index(b) + 1


XW = D + 1
ZR = WE // XW
NZ = (ROWS // P + ZR - 1) // ZR


def ahead(r, k, d):
    return r + (k + d) // RING, (k + d) % RING


def exists(r, k):
    return not isinstance(r, int) or 0 <= r < TURNS


def tile_loop(eng, step):
    for k in range(RING):
        step(0, k)
    with eng.Fori(1, TURNS - 1) as r:
        for k in range(RING):
            step(r, k)
    for k in range(RING):
        step(TURNS - 1, k)


def bass_xattn_moe(nc, x, ctxT, mask, wqkvo, bcols, bo, wg, bg, wffn, out):
    queue = nc.dram_tensor("queue", [ROWS, XW], F32, kind="Internal").ap()
    y_rows = nc.dram_tensor("y_rows", [2 + TOPK * B * T, D], F32, kind="Internal").ap()

    with ExitStack() as st:
        def sb(name, shape, dt=F32):
            return st.enter_context(nc.sbuf_tensor(name, shape, dt))

        def sem(name):
            return st.enter_context(nc.semaphore(name))

        bank = [st.enter_context(nc.psum_tensor(f"bank{i}", [P, 512], F32)) for i in range(8)]

        ident = sb("ident", [P, P])
        identR = sb("identR", [P, P], F32R)
        identB = sb("identB", [P, P], BF16)
        causal = sb("causal", [P, T], BF16)
        before = sb("before", [T, T], BF16)
        onesB = sb("onesB", [T, T], BF16)
        selKH = sb("selKH", [P, SLABS, 4, 4, DK], F32R)
        selKL = sb("selKL", [P, SLABS, 4, 4, DK], F32R)
        selQH = sb("selQH", [P, SLABS, 4, 4, DK], F32R)
        selQL = sb("selQL", [P, SLABS, 4, 4, DK], F32R)
        kbsel = sb("kbsel", [1, 4, 32], F32R)
        rind = sb("rind", [P, 32])
        group = sb("group", [P, 4])
        warm = sb("warm", [1, 1])
        kones = sb("kones", [P, 1])
        mhalf = sb("mhalf", [T, B])
        expert = sb("expert", [T, E])
        qbase = sb("qbase", [1, E])
        qbaseB = sb("qbaseB", [1, E], BF16)
        ids = sb("ids", [T, B, TOPK], I32)
        thr = sb("thr", [1, E, NJ])
        upto = sb("upto", [1, E, E])
        tile_no = sb("tile_no", [1, TILES, E])
        xin = sb("xin", [T, B, D])
        xbo = sb("xbo", [T, B, D])
        cxT = sb("cxT", [P, B, T])
        mraw = sb("mraw", [1, B, T], I32)
        kbias = sb("kbias", [1, B, T], F32R)
        w4 = sb("w4", [P, 4, D])
        bc = sb("bc", [P, 3])
        bo_b = sb("bo_b", [T, D])
        bg_row = sb("bg_row", [1, E])
        ones1 = sb("ones1", [1, T])
        wg_sb = sb("wg_sb", [P, E])
        wf = sb("wf", [P, E, WE])
        zrow = wf[:, E - 1, 0:ZR * XW]
        stats = sb("stats", [T, B, 6])
        mv = sb("mv", [T, B, 2])
        veps = sb("veps", [T, B])
        rstd = sb("rstd", [T, B])
        xn = sb("xn", [P, B, D])
        xnT = sb("xnT", [P, CT])
        kf = sb("kf", [P, CT])
        qf = sb("qf", [P, CT])
        kh = sb("kh", [P, CT], F32R)
        kl = sb("kl", [P, CT], F32R)
        qh = sb("qh", [P, CT], F32R)
        ql = sb("ql", [P, CT], F32R)
        Ks = sb("Ks", [P, B, SLABS, T], F32R)
        Qs = sb("Qs", [P, B, SLABS, T], F32R)
        Kd = sb("Kd", [P, CH, SLABS, 4, T], F32R)
        Qd = sb("Qd", [P, 2, SLABS, 4, T], F32R)
        Va = sb("Va", [P, B, H, 32])
        mx = sb("mx", [T, SLABS, 4])
        mn = sb("mn", [T, SLABS, 4])
        Mp = sb("Mp", [P, 2, SLABS, 4, 32], F32R)
        PT = sb("PT", [P, 2, SLABS, 4, T])
        Tsb = sb("Tsb", [P, 2, SLABS, T])
        rden = sb("rden", [T, H])
        ctxn = sb("ctxn", [T, D])
        coT = sb("coT", [P, T])
        x1 = sb("x1", [T, 2, D])
        stats2 = sb("stats2", [T, 6])
        mv2 = sb("mv2", [T, 2])
        veps2 = sb("veps2", [T, 1])
        rstd2 = sb("rstd2", [T, 1])
        xn2 = sb("xn2", [T, 4, D])
        base = sb("base", [T, B, D])
        xn2T = sb("xn2T", [P, T])
        top = sb("top", [T, 8])
        topi = sb("topi", [T, 8], U32)
        dlt = sb("dlt", [T, TOPK])
        ex = sb("ex", [T, TOPK])
        rd2 = sb("rd2", [T, 1])
        den = sb("den", [T, 1])
        wt = sb("wt", [T, 2, TOPK])
        M = sb("M", [T, TOPK, E])
        Ms = sb("Ms", [T, E], BF16)
        Mprev = sb("Mprev", [T, E], BF16)
        pr = sb("pr", [T, TOPK, E])
        ps = sb("ps", [T, TOPK])
        pos = sb("pos", [T, 2, TOPK], I32)
        xs = sb("xs", [T, 2, TOPK, XW])
        cmp7 = sb("cmp7", [1, E, NJ])
        tiles = sb("tiles", [1, E])
        tpre = sb("tpre", [1, E, E])
        tend = sb("tend", [1, E])
        cmpt = sb("cmpt", [1, TILES, E])
        tcnt = sb("tcnt", [1, TILES])
        skip = sb("skip", [1, E])
        cmps = sb("cmps", [1, TILES, E + 1])
        trow = sb("trow", [1, TILES])
        yrow = sb("yrow", [P, RING], I32)
        row_tab = sb("row_tab", [1, TILES], I32)
        exp_tab = sb("exp_tab", [1, TILES], I32)
        room = Va[:].rearrange("p b h r -> p (b h r)")
        sg = room[:, 0:2 * F].rearrange("p (a n) -> p a n", a=2)
        hT = room[:, 2 * F:4 * F].rearrange("p (a n) -> p a n", a=2)
        w1c = room[:, 4 * F:6 * F].rearrange("p (a n) -> p a n", a=2)
        xgT = room[:, 6 * F:6 * F + 2 * P].rearrange("p (a n) -> p a n", a=2)
        ysb = room[:, 6 * F + 2 * P:6 * F + 2 * P + 2 * D].rearrange("p (a n) -> p a n", a=2)
        w3c = xn[:].rearrange("p b d -> p (b d)").rearrange("p (a n) -> p a n", a=2)
        room2 = PT[:].rearrange("p a s c t -> p (a s c t)")
        xg = room2[:, 0:RING * XW].rearrange("p (a n) -> p a n", a=RING)
        yin = room2[0:T, RING * XW:RING * XW + TOPK * B * D].rearrange("p (s b d) -> p s b d", s=TOPK, b=B)
        fin = xin

        x_in, w_in, bc_in, b_in, wf_in, zfill = ([sem("x_in0"), sem("x_in1")], sem("w_in"), sem("bc_in"), sem("b_in"),
                                                 sem("wf_in"), sem("zfill"))
        ctx_in = [sem("ctx_in0"), sem("ctx_in1")]
        scat, y_out = [sem("scat0"), sem("scat1")], [sem("y_out0"), sem("y_out1")]
        y_in, o_out = [sem("y_in0"), sem("y_in1")], sem("o_out")
        tile_in = [sem(f"tile_in{k}") for k in range(RING)]
        pool_c, dve_c, c_id, z_c, v_c = sem("pool_c"), sem("dve_c"), sem("c_id"), sem("z_c"), sem("v_c")
        names = ("ln_st ln_ag ln_ve ln_rs xn_r prep_ps prep_A prep_V kh_r kl_r qh_r ql_r Kd_V Kd_A "
                 "s1_ps max_r mh_r ml_r qa_ps qa_r s2_ps exp_r p_r pv_ps t_r tt_ps rd_r cn_r ct_ps "
                 "coT_r wo_ps x1_r l2_st l2_ag l2_ve l2_rs xn2_r x2T_ps x2T_r lg_ps top_r topi_r "
                 "dl_r ex_r rd2_r w_r M_r Ms_r mp_r rk_ps pr_r ps_r pos_r xs_r id_r xbo_r cnt_ps "
                 "tab_s tab_r base_r gT_ps gT_r w1c_r w3c_r a_ps b_ps sg_r h_r y_ps ys_r fin_a fin_r").split()
        S = {n: sem(n) for n in names}

        block = st.enter_context(nc.Block())

        def spread(eng, b):
            wait_step(eng, step_no(b // CH, "Ks", SLABS - 1))
            eng.wait_ge(dve_c, 4)
            if b >= CH:
                eng.wait_ge(S["s1_ps"], SLABS * (b - CH + 1))
            for c in range(4):
                to, keys = Kd[:, b % CH, :, c, :], Ks[:, b].bitcast(F32)
                if spread_by(b)[0] == "V":
                    m = eng.tensor_scalar(to, keys, group[:, c:c + 1], None, ALU.mult)
                else:
                    m = eng.activation(to, keys, ACT.Copy, scale=group[:, c:c + 1])
            m.then_inc(S["Kd_" + spread_by(b)[0]], 1)

        def wait_step(eng, n):
            who, count = taken_out(n)
            eng.wait_ge(S["prep_" + who], count)

        @block.sync
        def _(sp):
            xv = x.rearrange("b t d -> t b d")
            for g in range(2):
                sp.dma_start(xin[:, g * CH:(g + 1) * CH, :], xv[:, g * CH:(g + 1) * CH, :]).then_inc(x_in[g], 16)
                if g == 0:
                    sp.dma_start(w4[:], wqkvo).then_inc(w_in, 16)
            sp.dma_start(cxT[:, CH:B, :], ctxT[:, CH:B, :]).then_inc(ctx_in[1], 16)
            sp.dma_start(bo_b[:], bo.rearrange("(a n) -> a n", a=1).broadcast_to([T, D])).then_inc(b_in, 16)
            sp.dma_start(bg_row[:], bg.rearrange("(a n) -> a n", a=1)).then_inc(b_in, 16)
            sp.dma_start(wg_sb[:], wg).then_inc(b_in, 16)
            sp.wait_ge(z_c, 1)
            zv = queue.rearrange("(p r) c -> p (r c)", p=P)
            per = ROWS // P
            for a in range(0, per, ZR):
                k = min(ZR, per - a)
                sp.dma_start(zv[:, a * XW:(a + k) * XW], zrow[:, 0:k * XW]).then_inc(zfill, 16)
            for e in range(E):
                if e == E - 1:
                    sp.wait_ge(zfill, 16 * NZ)
                sp.dma_start(wf[:, e, :], wffn[:, e, :]).then_inc(wf_in, 16)
            sp.wait_ge(S["tab_r"], 2)

            def load(r, k):
                row = sp.value_load(row_tab[0:1, bass.ds(RING * r + k, 1)], min_val=0, max_val=TRASH)
                if not exists(*ahead(r, k, -1)):
                    sp.wait_ge(scat[0], 16 * TOPK * B // 2)
                    sp.wait_ge(scat[1], 16 * TOPK * B // 2)
                if exists(*ahead(r, k, -RING)):
                    sp.wait_ge(S["gT_r"], RING * r + k - RING + 1)
                sp.dma_start(xg[:, k, :], queue[bass.ds(row, SLOT), :]).then_inc(tile_in[k], 16)

            tile_loop(sp, load)
            for c in range(2):
                sp.wait_ge(y_out[c], 16 * TILES // 2)
            yv = y_rows[2:2 + TOPK * B * T, :].rearrange("(s b t) d -> t s b d", s=TOPK, b=B)
            for c in range(2):
                bs = slice(c * B // 2, (c + 1) * B // 2)
                for s in range(TOPK):
                    sp.dma_start(yin[:, s, bs, :], yv[:, s, bs, :]).then_inc(y_in[c], 16)
            ov = out.rearrange("b t d -> t b d")
            for c in range(2):
                bs = slice(c * B // 2, (c + 1) * B // 2)
                sp.wait_ge(S["fin_r"], c + 1)
                sp.dma_start(ov[:, bs, :], fin[:, bs, :]).then_inc(o_out, 16)
            sp.wait_ge(o_out, 32)

        @block.gpsimd
        def _(g):
            g.memset(ident[:], 0.0).then_inc(c_id, 1)
            g.memset(mhalf[:], -0.5).then_inc(c_id, 1)
            g.wait_ge(c_id, 1)
            g.affine_select(out=ident[:], in_=ident[:], compare_op=ALU.not_equal, fill=1.0, base=0,
                            pattern=[[-1, P]], channel_multiplier=1).then_inc(c_id, 1)
            g.memset(causal[:], 0.0).then_inc(c_id, 1)
            g.memset(onesB[:], 1.0).then_inc(c_id, 1)
            g.memset(zrow, 0.0).then_inc(z_c, 1)

            def ln1_pow(g0):
                g.wait_ge(S["ln_ve"], g0 + 1)
                bs = slice(g0 * CH, (g0 + 1) * CH)
                g.tensor_tensor(rstd[:, bs], veps[:, bs], mhalf[:, bs], ALU.pow).then_inc(S["ln_rs"], 1)

            g.wait_ge(c_id, 5)
            ln1_pow(0)
            g.affine_select(out=causal[:], in_=causal[:], compare_op=ALU.is_ge, fill=BIG, base=0,
                            pattern=[[-1, T]], channel_multiplier=1).then_inc(pool_c, 1)
            g.affine_select(out=before[:], in_=onesB[:], compare_op=ALU.is_gt, fill=0.0, base=0,
                            pattern=[[1, T]], channel_multiplier=-1).then_inc(pool_c, 1)
            g.iota(qbase[:], pattern=[[PER_E, E]], base=-TRASH, channel_multiplier=0,
                   allow_small_or_imprecise_dtypes=True).then_inc(pool_c, 1)
            g.memset(ones1[:], 1.0).then_inc(pool_c, 1)
            g.memset(Mp[:].bitcast(U32), 0).then_inc(pool_c, 1)
            g.memset(Va[:, :, :, V_ONE:], 0.0).then_inc(v_c, 1)
            ln1_pow(1)
            g.wait_ge(v_c, 1)
            g.memset(Va[:, :, :, V_ONE:V_ONE + 1], 1.0).then_inc(pool_c, 1)
            g.iota(expert[:], pattern=[[1, E]], base=0, channel_multiplier=0,
                   allow_small_or_imprecise_dtypes=True).then_inc(pool_c, 1)
            g.iota(ids[:], pattern=[[T, B], [B * T, TOPK]], base=2, channel_multiplier=1).then_inc(pool_c, 1)
            g.iota(thr[:], pattern=[[0, E], [SLOT, NJ]], base=0, channel_multiplier=0,
                   allow_small_or_imprecise_dtypes=True).then_inc(pool_c, 1)
            g.iota(tile_no[:], pattern=[[1, TILES], [0, E]], base=0, channel_multiplier=0,
                   allow_small_or_imprecise_dtypes=True).then_inc(pool_c, 1)
            g.iota(cmps[:, :, E:E + 1], pattern=[[SLOT, TILES], [0, 1]], base=0, channel_multiplier=0,
                   allow_small_or_imprecise_dtypes=True).then_inc(pool_c, 1)
            g.memset(upto[:], 1.0).then_inc(v_c, 1)
            g.wait_ge(v_c, 2)
            g.affine_select(out=upto[:], in_=upto[:], compare_op=ALU.is_ge, fill=0.0, base=0,
                            pattern=[[1, E], [-1, E]], channel_multiplier=0).then_inc(pool_c, 1)

            def ln2_pow(b):
                g.wait_ge(S["l2_ve"], b + 1)
                g.tensor_tensor(rstd2[:], veps2[:], mhalf[:, 0:1], ALU.pow).then_inc(S["l2_rs"], 1)

            def keep_causal(b, u):
                g.wait_ge(S["exp_r"], 2 * b + u + 1)
                v = PT[0:T, b % 2, 2 * u:2 * u + 2].rearrange("p s c t -> p (s c) t")
                g.affine_select(out=v, in_=v, compare_op=ALU.is_ge, fill=0.0, base=0,
                                pattern=[[0, HG], [1, T]], channel_multiplier=-1).then_inc(S["p_r"], 1)

            def residual(b):
                g.wait_ge(S["xn2_r"], b + 1)
                g.tensor_tensor(base[:, b, :], x1[:, b % 2, :], xn2[:, b % 4, :], ALU.add).then_inc(S["base_r"], 1)

            def send(b):
                if b >= 2:
                    g.wait_ge(scat[b % 2], 16 * TOPK * (b // 2))
                g.tensor_copy(xs[:, b % 2, :, D:D + 1].bitcast(I32), ids[:, b, :].unsqueeze(2)).then_inc(S["id_r"], 1)
                g.wait_ge(S["id_r"], b + 1)
                g.wait_ge(S["xs_r"], TOPK * (b + 1))
                g.wait_ge(S["pos_r"], b + 1)
                if b == 0:
                    g.wait_ge(zfill, 16 * NZ)
                for s in range(TOPK):
                    g.indirect_dma_start(queue[:, :], bass.IndirectOffsetOnAxis(ap=pos[:, b % 2, s:s + 1], axis=0),
                                         xs[:, b % 2, s, :], None).then_inc(scat[b % 2], 16)

            g.wait_ge(b_in, 48)
            g.wait_ge(x_in[1], 16)
            for i in range(B + 4):
                now, scored, tail, routing, placing = i < B, 1 <= i <= B, 0 <= i - 2 < B, 0 <= i - 3 < B, 0 <= i - 4
                if placing and i > B:
                    send(i - 4)
                if routing:
                    residual(i - 3)
                if scored:
                    keep_causal(i - 1, 0)
                if scored:
                    keep_causal(i - 1, 1)
                if tail:
                    ln2_pow(i - 2)
                if placing and i <= B:
                    send(i - 4)
                if now:
                    g.tensor_tensor(xbo[:, i, :], xin[:, i, :], bo_b[:], ALU.add).then_inc(S["xbo_r"], 1)

            for t in range(TILES):
                g.wait_ge(S["ys_r"], t + 1)
                if t >= 2:
                    g.wait_ge(y_out[t % 2], 16 * (t // 2))
                g.indirect_dma_start(y_rows[:, :], bass.IndirectOffsetOnAxis(ap=yrow[:, t % RING:t % RING + 1], axis=0),
                                     ysb[:, t % 2, :], None).then_inc(y_out[t % 2], 16)

        @block.scalar
        def _(a):
            a.dma_start(cxT[:, 0:CH, :], ctxT[:, 0:CH, :]).then_inc(ctx_in[0], 16)
            a.dma_start(bc[:], bcols).then_inc(bc_in, 16)
            a.dma_start(mraw[:], mask.rearrange("(a b) t -> a b t", a=1)).then_inc(bc_in, 16)
            a.wait_ge(c_id, 3)
            a.activation(warm[:], ident[0:1, 0:1], ACT.Exp)
            a.wait_ge(bc_in, 32)

            def take_out(g0, kind, k=0):
                n = step_no(g0, kind, k)
                a.wait_ge(S["prep_ps"], n + 1)
                src = bank[BANKS[n]][:, 0:CT]
                if kind == "xT":
                    ins = a.activation(xnT[:], src, ACT.Copy)
                elif kind == "K":
                    ins = a.activation(kf[:], src, ACT.Identity, bias=bc[:, 0:1])
                elif kind == "Q":
                    ins = a.activation(qf[:], src, ACT.Identity, bias=bc[:, 1:2])
                else:
                    a.wait_ge(dve_c, 3)
                    dst, ones = (Ks, kones) if kind == "Ks" else (Qs, rind[:, R_KB:R_KB + 1])
                    ins = a.activation(dst[:, g0 * CH:(g0 + 1) * CH, k, :], src.rearrange("p (b t) -> p b t", b=CH),
                                       ACT.Identity, bias=ones[:, 0:1])
                ins.then_inc(S["prep_A"], 1)

            def qaug_evac(b):
                a.wait_ge(S["qa_ps"], b + 1)
                for c in range(4):
                    m = a.activation(Qd[:, b % 2, :, c, :], bank[4][:, 0:SLABS * T].rearrange("p (s t) -> p s t", s=SLABS),
                                     ACT.Copy, scale=group[:, c:c + 1])
                m.then_inc(S["qa_r"], 1)

            def exps(b, u):
                a.wait_ge(S["s2_ps"], 2 * b + u + 1)
                if b >= 2:
                    a.wait_ge(S["pv_ps"], 2 * (b - 2) + u + 1)
                for j in range(2):
                    m = a.activation(PT[0:T, b % 2, 2 * u + j],
                                     bank[2 + j][0:T, 0:4 * T].rearrange("p (c t) -> p c t", c=4), ACT.Exp,
                                     scale=SCALE)
                m.then_inc(S["exp_r"], 1)

            def t_evac(b):
                a.wait_ge(S["pv_ps"], 2 * b + 2)
                a.activation(Tsb[:, b % 2], bank[5][:, 0:SLABS * T].rearrange("p (s t) -> p s t", s=SLABS),
                             ACT.Copy).then_inc(S["t_r"], 1)

            def coT_evac(b):
                a.wait_ge(S["ct_ps"], b + 1)
                a.activation(coT[:], bank[7][:, 0:T], ACT.Identity, bias=bc[:, 2:3]).then_inc(S["coT_r"], 1)

            def route(b):
                a.wait_ge(S["dl_r"], b + 1)
                a.activation(ex[:], dlt[:], ACT.Exp, accum_out=den[:]).then_inc(S["ex_r"], 1)

            def scale_rows(b):
                a.wait_ge(S["w_r"], b + 1)
                if b >= 2:
                    a.wait_ge(scat[b % 2], 16 * TOPK * (b // 2))
                for s in range(TOPK):
                    a.activation(xs[:, b % 2, s, 0:D], xn2[:, b % 4, :], ACT.Copy,
                                 scale=wt[:, b % 2, s:s + 1]).then_inc(S["xs_r"], 1)

            for kind, k, eng in STEPS[0:NSTEP]:
                if eng == "A":
                    take_out(0, kind, k)
            for i in range(B + 4):
                now, scored, tail, routing, placing = i < B, 1 <= i <= B, 0 <= i - 2 < B, 0 <= i - 3 < B, 0 <= i - 4
                if scored:
                    exps(i - 1, 0)
                for kind, k, eng in beside(i, 0):
                    if eng == "A":
                        take_out(1, kind, k)
                if tail:
                    coT_evac(i - 2)
                if scored:
                    exps(i - 1, 1)
                for kind, k, eng in beside(i, 1):
                    if eng == "A":
                        take_out(1, kind, k)
                if routing:
                    route(i - 3)
                if now:
                    qaug_evac(i)
                for kind, k, eng in beside(i, 2):
                    if eng == "A":
                        take_out(1, kind, k)
                if scored:
                    t_evac(i - 1)
                if routing:
                    scale_rows(i - 3)
                for b in SPREADS_A.get(i, ()):
                    spread(a, b)

            wrow = wf[:].rearrange("p e n -> p (e n)")

            def fetch_w1(r, k):
                e = a.value_load(exp_tab[0:1, bass.ds(RING * r + k, 1)], min_val=0, max_val=(E - 1) * WE)
                if exists(*ahead(r, k, -2)):
                    a.wait_ge(S["a_ps"], RING * r + k - 1)
                a.activation(w1c[:, k % 2, :], wrow[:, bass.ds(e, F)], ACT.Copy).then_inc(S["w1c_r"], 1)

            def silu(r, k):
                a.wait_ge(S["a_ps"], RING * r + k + 1)
                if exists(*ahead(r, k, -2)):
                    a.wait_ge(S["h_r"], RING * r + k - 1)
                a.activation(sg[:, k % 2, :], bank[1 + k % 2][:], ACT.Silu).then_inc(S["sg_r"], 1)

            def tile_step(r, k):
                silu(r, k)
                if exists(*ahead(r, k, 2)):
                    fetch_w1(*ahead(r, k, 2))

            a.wait_ge(wf_in, 16 * E)
            a.wait_ge(S["tab_r"], 1)
            fetch_w1(0, 0)
            fetch_w1(0, 1)
            tile_loop(a, tile_step)

        @block.tensor
        def _(pe):
            pe.wait_ge(c_id, 3)

            def prepare(g0, kind, k=0):
                n = step_no(g0, kind, k)
                if step_before(n) is not None:
                    wait_step(pe, step_before(n))
                o = bank[BANKS[n]]
                flat = "p c j d -> p (c j d)"
                if kind == "xT":
                    pe.wait_ge(S["xn_r"], g0 + 1)
                    for b in range(CH):
                        m = pe.transpose(o[:, b * T:(b + 1) * T], xn[0:T, g0 * CH + b, :], ident[0:T, 0:T])
                elif kind == "K":
                    pe.wait_ge(ctx_in[g0], 16)
                    pe.wait_ge(w_in, 16)
                    m = pe.matmul(o[:, 0:CT], w4[:, 1, :], cxT[:, g0 * CH:(g0 + 1) * CH, :].rearrange("p b t -> p (b t)"),
                                  start=True, stop=True)
                elif kind == "Q":
                    wait_step(pe, step_no(g0, "xT"))
                    m = pe.matmul(o[:, 0:CT], w4[:, 0, :], xnT[:], start=True, stop=True)
                elif kind == "V":
                    for b in range(2):
                        m = pe.matmul(o[0:T, b * D:(b + 1) * D], cxT[:, g0 * CH + 2 * k + b, :], w4[:, 2, :],
                                      start=True, stop=True)
                elif kind == "Ks":
                    pe.wait_ge(S["kl_r"], g0 + 1)
                    pe.wait_ge(dve_c, 3)
                    pe.matmul(o[:, 0:CT], selKH[:, k].rearrange(flat), kh[:], start=True, stop=False)
                    pe.matmul(o[:, 0:CT], selKL[:, k].rearrange(flat), kl[:], start=False, stop=False)
                    m = pe.matmul(o[:, 0:CT], kbsel[:].rearrange("p c r -> p (c r)"),
                                  kbias[:, g0 * CH:(g0 + 1) * CH, :].rearrange("p b t -> p (b t)"),
                                  start=False, stop=True)
                else:
                    pe.wait_ge(S["ql_r"], g0 + 1)
                    pe.matmul(o[:, 0:CT], selQH[:, k].rearrange(flat), qh[:], start=True, stop=False)
                    m = pe.matmul(o[:, 0:CT], selQL[:, k].rearrange(flat), ql[:], start=False, stop=True)
                m.then_inc(S["prep_ps"], 1)

            def s1(b, s):
                n = SLABS * b + s
                if n >= 2:
                    pe.wait_ge(S["max_r"], n - 1)
                o = bank[s % 2][0:T, 0:4 * T].rearrange("p (c t) -> p c t", c=4)
                pe.matmul(o, identB[:, 0:T], causal[:].unsqueeze(1).broadcast_to([P, 4, T]), start=True, stop=False)
                pe.matmul(o, Qs[:, b, s, :], Kd[:, b % CH, s], start=False, stop=True).then_inc(S["s1_ps"], 1)

            def place_queries(b):
                if b >= 1:
                    pe.wait_ge(S["qa_r"], b)
                pe.matmul(bank[4][:, 0:SLABS * T], identR[:], Qs[:, b].rearrange("p s t -> p (s t)"), start=True,
                          stop=False, skip_group_check=True)

            def place_max(b):
                pe.wait_ge(S["ml_r"], b + 1)
                for s in range(SLABS):
                    m = pe.matmul(bank[4][:, s * T:(s + 1) * T], Mp[:, b % 2, s].rearrange("p c r -> p (c r)"),
                                  identR[:, 0:T], start=False, stop=True, skip_group_check=True)
                m.then_inc(S["qa_ps"], 1)

            def s2(b, u):
                pe.wait_ge(S["qa_r"], b + 1)
                if 2 * b + u >= 1:
                    pe.wait_ge(S["exp_r"], 2 * b + u)
                for j in range(2):
                    s = 2 * u + j
                    m = pe.matmul(bank[2 + j][0:T, 0:4 * T], Ks[:, b, s, :],
                                  Qd[:, b % 2, s].rearrange("p c t -> p (c t)"), start=True, stop=True)
                m.then_inc(S["s2_ps"], 1)

            def pv(b, u):
                if b >= 1 and u == 0:
                    pe.wait_ge(S["t_r"], b)
                if u == 0 and b % CH == 0:
                    wait_step(pe, step_no(b // CH, "V", 1))
                    pe.wait_ge(pool_c, 6)
                if u == 0 and b == 0:
                    wait_step(pe, step_no(1, "V", 1))
                pe.wait_ge(S["p_r"], 2 * b + u + 1)
                for s in (2 * u, 2 * u + 1):
                    for c in range(4):
                        m = pe.matmul(bank[5][32 * c:32 * c + 32, s * T:(s + 1) * T], Va[0:T, b, 4 * s + c, :],
                                      PT[0:T, b % 2, s, c, :], start=True, stop=True)
                m.then_inc(S["pv_ps"], 1)

            def t_turn(b):
                pe.wait_ge(S["t_r"], b + 1)
                if b >= 1:
                    pe.wait_ge(S["x1_r"], b)
                else:
                    wait_step(pe, step_no(1, "Ks", 2))
                for s in range(SLABS):
                    m = pe.transpose(bank[7][0:T, s * P:(s + 1) * P], Tsb[:, b % 2, s, :], ident[:])
                m.then_inc(S["tt_ps"], 1)

            def ctx_turn(b):
                pe.wait_ge(S["cn_r"], b + 1)
                pe.transpose(bank[7][:, 0:T], ctxn[:], ident[0:T, 0:T]).then_inc(S["ct_ps"], 1)

            def wo(b):
                pe.wait_ge(S["coT_r"], b + 1)
                pe.matmul(bank[7][0:T, P:P + D], coT[:], w4[:, 3, :], start=True, stop=True).then_inc(S["wo_ps"], 1)

            def xn2_turn(b):
                pe.wait_ge(S["xn2_r"], b + 1)
                if b == 0:
                    wait_step(pe, 2 * NSTEP - 1)
                    pe.wait_ge(b_in, 48)
                else:
                    pe.wait_ge(S["pr_r"], b)
                pe.transpose(bank[6][:, 0:T], xn2[:, b % 4, :], ident[0:T, 0:T]).then_inc(S["x2T_ps"], 1)

            def logits(b):
                pe.wait_ge(S["x2T_r"], b + 1)
                pe.matmul(bank[6][0:T, 0:E], xn2T[:], wg_sb[:], start=True, stop=False)
                pe.matmul(bank[6][0:T, 0:E], ones1[:], bg_row[:], start=False, stop=True).then_inc(S["lg_ps"], 1)

            def rank(b):
                pe.wait_ge(S["Ms_r"], b + 1)
                if b >= 1:
                    pe.wait_ge(S["mp_r"], b)
                if b == 0:
                    pe.wait_ge(dve_c, 7)
                pe.matmul(bank[6][0:T, 0:E], onesB[0:1, :], qbaseB[:], start=True, stop=False)
                pe.matmul(bank[6][0:T, 0:E], before[:], Ms[:], start=False, stop=False)
                pe.matmul(bank[6][0:T, 0:E], onesB[:], Mprev[:], start=False, stop=True).then_inc(S["rk_ps"], 1)

            for kind, k, _ in STEPS[0:NSTEP]:
                prepare(0, kind, k)
            pe.wait_ge(pool_c, 1)
            for i in range(B + 4):
                now, scored, tail, routing, placing = i < B, 1 <= i <= B, 0 <= i - 2 < B, 0 <= i - 3 < B, 0 <= i - 4
                if i in (0, CH):
                    g0 = i // CH
                    wait_step(pe, step_no(g0, "Qs", 2))
                    wait_step(pe, step_no(g0, "Qs", 3))
                if now:
                    who, count = spread_by(i)
                    pe.wait_ge(S["Kd_" + who], count)
                    s1(i, 0)
                if now:
                    s1(i, 1)
                if tail:
                    t_turn(i - 2)
                if scored:
                    s2(i - 1, 0)
                for kind, k, _ in beside(i, 0):
                    prepare(1, kind, k)
                if now:
                    s1(i, 2)
                if routing:
                    xn2_turn(i - 3)
                if now:
                    s1(i, 3)
                if tail:
                    ctx_turn(i - 2)
                if routing:
                    logits(i - 3)
                if scored:
                    s2(i - 1, 1)
                for kind, k, _ in beside(i, 1):
                    prepare(1, kind, k)
                if now:
                    place_queries(i)
                if tail:
                    wo(i - 2)
                if scored:
                    pv(i - 1, 0)
                if now:
                    place_max(i)
                if routing:
                    rank(i - 3)
                for kind, k, _ in beside(i, 2):
                    prepare(1, kind, k)
                if scored:
                    pv(i - 1, 1)
            pe.matmul(bank[0][0:T, 0:E], onesB[:], Ms[:], start=True, stop=False)
            pe.matmul(bank[0][0:T, 0:E], onesB[:], Mprev[:], start=False, stop=True).then_inc(S["cnt_ps"], 1)

            def x_turn(r, k):
                pe.wait_ge(tile_in[k], 16 * (r + 1))
                if exists(*ahead(r, k, -1)):
                    pe.wait_ge(S["gT_r"], RING * r + k)
                pe.transpose(bank[0][:, 0:P], xg[:, k, 0:D], ident[:]).then_inc(S["gT_ps"], 1)

            def up(r, k):
                t = RING * r + k
                pe.wait_ge(S["gT_r"], t + 1)
                pe.wait_ge(S["w1c_r"], t + 1)
                if exists(*ahead(r, k, -2)):
                    pe.wait_ge(S["sg_r"], t - 1)
                for c in range(FC):
                    m = pe.matmul(bank[1 + k % 2][:, c * P:(c + 1) * P], w1c[:, k % 2, c * P:(c + 1) * P],
                                  xgT[:, k % 2, :], start=True, stop=True)
                m.then_inc(S["a_ps"], 1)
                pe.wait_ge(S["w3c_r"], t + 1)
                if exists(*ahead(r, k, -2)):
                    pe.wait_ge(S["h_r"], t - 1)
                for c in range(FC):
                    m = pe.matmul(bank[3 + 2 * (k % 2)][:, c * P:(c + 1) * P], w3c[:, k % 2, c * P:(c + 1) * P],
                                  xgT[:, k % 2, :], start=True, stop=True)
                m.then_inc(S["b_ps"], 1)

            def down(r, k, e):
                t = RING * r + k
                wrow = wf[:].rearrange("p e n -> p (e n)")
                pe.wait_ge(S["h_r"], t + 1)
                if exists(*ahead(r, k, -2)):
                    pe.wait_ge(S["ys_r"], t - 1)
                for c in range(FC):
                    m = pe.matmul(bank[4 + 3 * (k % 2)][:, 0:D], hT[:, k % 2, c * P:(c + 1) * P],
                                  wrow[:, bass.ds(e + 2 * F + c * D, D)], start=(c == 0), stop=(c == FC - 1))
                m.then_inc(S["y_ps"], 1)

            def tile_step(r, k):
                e = pe.value_load(exp_tab[0:1, bass.ds(RING * r + k, 1)], min_val=0, max_val=(E - 1) * WE)
                if exists(*ahead(r, k, 1)):
                    up(*ahead(r, k, 1))
                if exists(*ahead(r, k, 2)):
                    x_turn(*ahead(r, k, 2))
                down(r, k, e)

            pe.wait_ge(wf_in, 16 * E)
            pe.wait_ge(S["tab_r"], 1)
            x_turn(0, 0)
            up(0, 0)
            x_turn(0, 1)
            tile_loop(pe, tile_step)

        @block.vector
        def _(v):
            def ln1_stats(g0):
                v.wait_ge(x_in[g0], 16)
                for b in range(g0 * CH, (g0 + 1) * CH):
                    m = v.bn_stats(stats[:, b, :], xin[:, b, :])
                m.then_inc(S["ln_st"], 1)
                v.wait_ge(S["ln_st"], g0 + 1)
                for b in range(g0 * CH, (g0 + 1) * CH):
                    m = v.bn_aggr(mv[:, b, :], stats[:, b, :])
                m.then_inc(S["ln_ag"], 1)
                v.wait_ge(S["ln_ag"], g0 + 1)
                v.tensor_scalar(veps[:, g0 * CH:(g0 + 1) * CH], mv[:, g0 * CH:(g0 + 1) * CH, 1], EPS, None, ALU.add)\
                    .then_inc(S["ln_ve"], 1)

            def ln1_apply(g0):
                v.wait_ge(S["ln_rs"], g0 + 1)
                for b in range(g0 * CH, (g0 + 1) * CH):
                    m = v.tensor_scalar(xn[0:T, b, :], xin[:, b, :], mv[:, b, 0:1], rstd[:, b:b + 1], ALU.subtract, ALU.mult)
                m.then_inc(S["xn_r"], 1)

            def take_out(g0, kind, k=0):
                n = step_no(g0, kind, k)
                v.wait_ge(S["prep_ps"], n + 1)
                o = bank[BANKS[n]]
                if kind == "V":
                    b = g0 * CH + 2 * k
                    ins = v.tensor_copy(Va[0:T, b:b + 2, :, 0:DK],
                                        o[0:T, 0:2 * D].rearrange("p (b h d) -> p b h d", b=2, h=H))
                else:
                    ins = v.tensor_scalar(Qs[:, g0 * CH:(g0 + 1) * CH, k, :],
                                          o[:, 0:CT].rearrange("p (b t) -> p b t", b=CH), rind[:, R_KB:R_KB + 1], None,
                                          ALU.add)
                ins.then_inc(S["prep_V"], 1)

            def split_high(g0, full, high, kind, done):
                wait_step(v, step_no(g0, kind))
                v.tensor_copy(high[:], full[:]).then_inc(done, 1)

            def split_low(g0, full, high, low, ready, done):
                v.wait_ge(ready, g0 + 1)
                v.tensor_tensor(low[:], full[:], high[:].bitcast(F32), ALU.subtract).then_inc(done, 1)

            v.memset(selKH[:].bitcast(U32), 0)
            v.memset(selKL[:].bitcast(U32), 0)
            v.memset(selQH[:].bitcast(U32), 0)
            v.memset(selQL[:].bitcast(U32), 0)
            v.memset(kbsel[:].bitcast(U32), 0).then_inc(dve_c, 1)
            ln1_stats(0)
            v.wait_ge(c_id, 3)
            v.wait_ge(dve_c, 1)
            v.tensor_scalar(kbsel[:, :, R_KB:R_KB + 1], kbsel[:, :, R_KB:R_KB + 1].bitcast(F32), 1.0, None, ALU.add)
            iv = ident[:].rearrange("p (s c d) -> p s c d", s=SLABS, c=4)
            for j in (0, 2):
                v.tensor_copy(selKH[:, :, :, j, :], iv)
            v.tensor_copy(selKL[:, :, :, 1, :], iv)
            v.tensor_reduce(rind[:], ident[:].rearrange("p (c r) -> p r c", c=4), AX.X, ALU.add).then_inc(dve_c, 1)
            ln1_apply(0)
            v.wait_ge(dve_c, 2)
            v.tensor_tensor(kones[:], rind[:, R_MH:R_MH + 1], rind[:, R_ML:R_ML + 1], ALU.add)
            v.wait_ge(bc_in, 32)
            v.tensor_scalar(kbias[:], mraw[:], 0.0, BIG, ALU.is_equal, ALU.mult).then_inc(dve_c, 1)
            split_high(0, kf, kh, "K", S["kh_r"])
            split_low(0, kf, kh, kl, S["kh_r"], S["kl_r"])
            for j in (0, 1):
                v.tensor_copy(selQH[:, :, :, j, :], iv)
            v.tensor_copy(selQL[:, :, :, 2, :], iv)
            v.tensor_reduce(group[:], ident[:].rearrange("p (c r) -> p c r", c=4), AX.X, ALU.add).then_inc(dve_c, 1)
            split_high(0, qf, qh, "Q", S["qh_r"])
            split_low(0, qf, qh, ql, S["qh_r"], S["ql_r"])
            v.tensor_copy(identR[:], ident[:])
            v.tensor_copy(identB[:], ident[:]).then_inc(dve_c, 1)
            v.memset(dlt[:], 0.0)
            v.memset(Mprev[:], 0.0).then_inc(dve_c, 1)
            spread(v, 0)
            take_out(0, "Qs", 1)
            take_out(0, "Qs", 3)
            take_out(0, "V", 0)
            take_out(0, "V", 1)

            def maxima(b, s):
                v.wait_ge(S["s1_ps"], SLABS * b + s + 1)
                v.tensor_reduce(mx[:, s], bank[s % 2][0:T, 0:4 * T].rearrange("p (c t) -> p c t", c=4),
                                AX.X, ALU.max).then_inc(S["max_r"], 1)

            def negate_max(b):
                v.wait_ge(S["max_r"], 4 * b + 4)
                mp = Mp[0:T, b % 2]
                if b == 0:
                    v.wait_ge(pool_c, 5)
                if b >= 2:
                    v.wait_ge(S["qa_ps"], b - 1)
                v.tensor_scalar(mn[:], mx[:], -1.0, CLAMP, ALU.mult, ALU.min)
                v.tensor_scalar(mp[:, :, :, R_MH], mx[:], -1.0, CLAMP, ALU.mult, ALU.min).then_inc(S["mh_r"], 1)

            def negated_low(b):
                v.wait_ge(S["mh_r"], b + 1)
                mp = Mp[0:T, b % 2]
                v.tensor_tensor(mp[:, :, :, R_ML], mn[:], mp[:, :, :, R_MH].bitcast(F32), ALU.subtract)\
                    .then_inc(S["ml_r"], 1)

            def invert_sums(b):
                v.wait_ge(S["tt_ps"], b + 1)
                v.reciprocal(rden[:], bank[7][0:T, :].rearrange("p (h r) -> p h r", h=H)[:, :, V_ONE])\
                    .then_inc(S["rd_r"], 1)

            def norm(b):
                v.wait_ge(S["rd_r"], b + 1)
                o = bank[7][0:T, :].rearrange("p (h r) -> p h r", h=H)
                v.tensor_tensor(ctxn[:].rearrange("p (h d) -> p h d", h=H), o[:, :, 0:DK],
                                rden[:].unsqueeze(2).broadcast_to([T, H, DK]), ALU.mult).then_inc(S["cn_r"], 1)

            def add_x(b):
                v.wait_ge(S["wo_ps"], b + 1)
                v.wait_ge(S["xbo_r"], b + 1)
                if b >= 2:
                    v.wait_ge(S["base_r"], b - 1)
                v.tensor_tensor(x1[:, b % 2, :], bank[7][0:T, P:P + D], xbo[:, b, :], ALU.add).then_inc(S["x1_r"], 1)

            def ln2_stats(b):
                v.wait_ge(S["x1_r"], b + 1)
                v.bn_stats(stats2[:], x1[:, b % 2, :]).then_inc(S["l2_st"], 1)

            def ln2_mean(b):
                v.wait_ge(S["l2_st"], b + 1)
                v.bn_aggr(mv2[:], stats2[:]).then_inc(S["l2_ag"], 1)

            def ln2_guard(b):
                v.wait_ge(S["l2_ag"], b + 1)
                v.tensor_scalar(veps2[:], mv2[:, 1:2], EPS, None, ALU.add).then_inc(S["l2_ve"], 1)

            def ln2_apply(b):
                v.wait_ge(S["l2_rs"], b + 1)
                if b >= 4:
                    v.wait_ge(S["xs_r"], TOPK * (b - 3))
                v.tensor_scalar(xn2[:, b % 4, :], x1[:, b % 2, :], mv2[:, 0:1], rstd2[:], ALU.subtract, ALU.mult)\
                    .then_inc(S["xn2_r"], 1)

            def xn2T_evac(b):
                v.wait_ge(S["x2T_ps"], b + 1)
                v.tensor_copy(xn2T[:], bank[6][:, 0:T]).then_inc(S["x2T_r"], 1)

            def top_logits(b):
                v.wait_ge(S["lg_ps"], b + 1)
                v.max(top[:], bank[6][0:T, 0:E]).then_inc(S["top_r"], 1)

            def top_experts(b):
                v.wait_ge(S["top_r"], b + 1)
                v.max_index(topi[:], top[:], bank[6][0:T, 0:E]).then_inc(S["topi_r"], 1)
                v.tensor_tensor(dlt[:, 1:2], top[:, 1:2], top[:, 0:1], ALU.subtract).then_inc(S["dl_r"], 1)

            def one_hot(b):
                v.wait_ge(S["topi_r"], b + 1)
                v.tensor_tensor(M[:], expert[:].unsqueeze(1).broadcast_to([T, TOPK, E]),
                                topi[:, 0:TOPK].unsqueeze(2).broadcast_to([T, TOPK, E]), ALU.is_equal)\
                    .then_inc(S["M_r"], 1)
                if b >= 1:
                    v.wait_ge(S["rk_ps"], b)
                    v.tensor_tensor(Mprev[:], Mprev[:], Ms[:], ALU.add).then_inc(S["mp_r"], 1)

            def both_experts(b):
                v.wait_ge(S["M_r"], b + 1)
                if b >= 1:
                    v.wait_ge(S["mp_r"], b)
                v.tensor_tensor(Ms[:], M[:, 0, :], M[:, 1, :], ALU.add).then_inc(S["Ms_r"], 1)

            def invert_den(b):
                v.wait_ge(S["ex_r"], b + 1)
                v.reciprocal(rd2[:], den[:]).then_inc(S["rd2_r"], 1)

            def weigh(b):
                v.wait_ge(S["rd2_r"], b + 1)
                if b >= 2:
                    v.wait_ge(S["xs_r"], TOPK * (b - 1))
                v.tensor_scalar(wt[:, b % 2, :], ex[:], rd2[:], None, ALU.mult).then_inc(S["w_r"], 1)

            def pick_rank(b):
                v.wait_ge(S["rk_ps"], b + 1)
                v.tensor_tensor(pr[:], M[:], bank[6][0:T, 0:E].unsqueeze(1).broadcast_to([T, TOPK, E]), ALU.mult)\
                    .then_inc(S["pr_r"], 1)

            def sum_rank(b):
                v.wait_ge(S["pr_r"], b + 1)
                v.tensor_reduce(ps[:], pr[:], AX.X, ALU.add).then_inc(S["ps_r"], 1)

            def place(b):
                v.wait_ge(S["ps_r"], b + 1)
                if b >= 2:
                    v.wait_ge(scat[b % 2], 16 * TOPK * (b // 2))
                v.tensor_scalar(pos[:, b % 2, :], ps[:], float(TRASH), None, ALU.add).then_inc(S["pos_r"], 1)

            for i in range(B + 3):
                now, scored, tail, routing, placing = i < B, 1 <= i <= B, 0 <= i - 2 < B, 0 <= i - 3 < B, 0 <= i - 4
                if now:
                    maxima(i, 0)
                if placing:
                    pick_rank(i - 4)
                if routing:
                    ln2_apply(i - 3)
                if placing:
                    sum_rank(i - 4)
                if now:
                    maxima(i, 1)
                if i == 0:
                    ln1_stats(1)
                if i == 3:
                    take_out(1, "Qs", 3)
                if placing:
                    place(i - 4)
                if tail:
                    invert_sums(i - 2)
                if routing:
                    xn2T_evac(i - 3)
                if tail:
                    norm(i - 2)
                if now:
                    maxima(i, 2)
                if routing:
                    top_logits(i - 3)
                if now:
                    maxima(i, 3)
                if routing:
                    top_experts(i - 3)
                if now:
                    negate_max(i)
                if routing:
                    one_hot(i - 3)
                if now:
                    negated_low(i)
                if routing:
                    both_experts(i - 3)
                if i == 0:
                    ln1_apply(1)
                    spread(v, 1)
                    split_high(1, kf, kh, "K", S["kh_r"])
                    split_low(1, kf, kh, kl, S["kh_r"], S["kl_r"])
                if i == 1:
                    split_high(1, qf, qh, "Q", S["qh_r"])
                    split_low(1, qf, qh, ql, S["qh_r"], S["ql_r"])
                    v.wait_ge(pool_c, 12)
                    v.wait_ge(dve_c, 6)
                    v.tensor_copy(qbaseB[:], qbase[:]).then_inc(dve_c, 1)
                if i == 0:
                    take_out(1, "V", 0)
                    take_out(1, "V", 1)
                if routing:
                    invert_den(i - 3)
                if i == 2:
                    take_out(1, "Qs", 1)
                if tail:
                    add_x(i - 2)
                if routing:
                    weigh(i - 3)
                if tail:
                    ln2_stats(i - 2)
                for b in SPREADS_V.get(i, ()):
                    spread(v, b)
                if tail:
                    ln2_mean(i - 2)
                if tail:
                    ln2_guard(i - 2)
            def wait_table(n):
                v.wait_ge(S["tab_s"], n)

            pick_rank(B - 1)
            v.wait_ge(S["cnt_ps"], 1)
            v.tensor_tensor(cmp7[:], bank[0][0:1, 0:E].unsqueeze(2).broadcast_to([1, E, NJ]), thr[:], ALU.is_gt)\
                .then_inc(S["tab_s"], 1)
            sum_rank(B - 1)
            wait_table(1)
            v.tensor_reduce(tiles[:], cmp7[:], AX.X, ALU.add).then_inc(S["tab_s"], 1)
            place(B - 1)
            wait_table(2)
            v.tensor_tensor(tpre[:], tiles[:].unsqueeze(1).broadcast_to([1, E, E]), upto[:], ALU.mult)\
                .then_inc(S["tab_s"], 1)
            v.tensor_scalar(skip[:], tiles[:], -float(SLOT), float(PER_E), ALU.mult, ALU.add).then_inc(S["tab_s"], 1)
            wait_table(3)
            v.tensor_reduce(tend[:], tpre[:], AX.X, ALU.add).then_inc(S["tab_s"], 1)
            wait_table(5)
            v.tensor_tensor(cmpt[:], tend[:].unsqueeze(1).broadcast_to([1, TILES, E]), tile_no[:], ALU.is_le)\
                .then_inc(S["tab_s"], 1)
            wait_table(6)
            v.tensor_tensor(cmps[:, :, 0:E], skip[:].unsqueeze(1).broadcast_to([1, TILES, E]), cmpt[:], ALU.mult)\
                .then_inc(S["tab_s"], 1)
            v.tensor_reduce(tcnt[:], cmpt[:], AX.X, ALU.add).then_inc(S["tab_s"], 1)
            wait_table(7)
            v.tensor_reduce(trow[:], cmps[:], AX.X, ALU.add).then_inc(S["tab_s"], 1)
            wait_table(8)
            v.tensor_scalar(exp_tab[:], tcnt[:], float(E - 1), float(WE), ALU.min, ALU.mult).then_inc(S["tab_r"], 1)
            wait_table(9)
            v.tensor_scalar(row_tab[:], trow[:], float(TRASH), None, ALU.min).then_inc(S["tab_r"], 1)

            def gT_evac(r, k):
                v.wait_ge(S["gT_ps"], RING * r + k + 1)
                if exists(*ahead(r, k, -2)):
                    v.wait_ge(S["b_ps"], RING * r + k - 1)
                v.tensor_scalar(yrow[:, k:k + 1], xg[:, k, D:D + 1].bitcast(I32), float(k % 2), None, ALU.max)
                v.tensor_copy(xgT[:, k % 2, :], bank[0][:, 0:P]).then_inc(S["gT_r"], 1)

            wrow = wf[:].rearrange("p e n -> p (e n)")

            def fetch_w3(r, k):
                e = v.value_load(exp_tab[0:1, bass.ds(RING * r + k, 1)], min_val=0, max_val=(E - 1) * WE)
                if exists(*ahead(r, k, -2)):
                    v.wait_ge(S["b_ps"], RING * r + k - 1)
                v.tensor_copy(w3c[:, k % 2, :], wrow[:, bass.ds(e + F, F)]).then_inc(S["w3c_r"], 1)

            def gate(r, k):
                v.wait_ge(S["sg_r"], RING * r + k + 1)
                v.wait_ge(S["b_ps"], RING * r + k + 1)
                if exists(*ahead(r, k, -2)):
                    v.wait_ge(S["y_ps"], RING * r + k - 1)
                v.tensor_tensor(hT[:, k % 2, :], sg[:, k % 2, :], bank[3 + 2 * (k % 2)][:], ALU.mult).then_inc(S["h_r"], 1)

            def y_evac(r, k):
                v.wait_ge(S["y_ps"], RING * r + k + 1)
                if exists(*ahead(r, k, -2)):
                    v.wait_ge(y_out[k % 2], 16 * (RING // 2 * r + k // 2))
                v.tensor_copy(ysb[:, k % 2, :], bank[4 + 3 * (k % 2)][:, 0:D]).then_inc(S["ys_r"], 1)

            def tile_step(r, k):
                gate(r, k)
                if exists(*ahead(r, k, 2)):
                    fetch_w3(*ahead(r, k, 2))
                if exists(*ahead(r, k, -1)):
                    y_evac(*ahead(r, k, -1))
                if exists(*ahead(r, k, 2)):
                    if exists(*ahead(r, k, -2)):
                        v.wait_ge(y_out[k % 2], 16 * (RING // 2 * r + k // 2))
                    gT_evac(*ahead(r, k, 2))

            v.wait_ge(wf_in, 16 * E)
            v.wait_ge(S["tab_r"], 1)
            fetch_w3(0, 0)
            fetch_w3(0, 1)
            gT_evac(0, 0)
            gT_evac(0, 1)
            tile_loop(v, tile_step)
            y_evac(TURNS - 1, RING - 1)
            for c in range(2):
                bs = slice(c * B // 2, (c + 1) * B // 2)
                v.wait_ge(y_in[c], 16 * TOPK)
                v.wait_ge(S["base_r"], B)
                v.tensor_tensor(fin[:, bs, :], yin[:, 0, bs, :], yin[:, 1, bs, :], ALU.add).then_inc(S["fin_a"], 1)
                v.wait_ge(S["fin_a"], c + 1)
                v.tensor_tensor(fin[:, bs, :], fin[:, bs, :], base[:, bs, :], ALU.add).then_inc(S["fin_r"], 1)


def kernel(**inputs):
    import numpy as np
    import concourse.bacc as bacc
    from concourse.bass_utils import run_bass_kernel_spmd

    i = {k: np.asarray(v) for k, v in inputs.items()}
    w = [i["L0_xattn_" + n] for n in ("Wq", "Wk", "Wv", "Wo")]
    e13 = np.stack([i["L0_ffn_W1"], i["L0_ffn_W3"]], axis=2)
    e2 = i["L0_ffn_W2"].reshape(E, FC, P, D).transpose(2, 0, 1, 3)
    arrays = {
        "x": i["x"],
        "ctxT": i["ctx_1024"][:, :T, :].transpose(2, 0, 1),
        "mask": i["mask_BxS2_if1"][:, :T],
        "wqkvo": np.stack([a.T for a in w], axis=1),
        "bcols": np.stack([i["L0_xattn_bk"], i["L0_xattn_bq"], i["L0_xattn_bv"]], axis=1),
        "bo": i["L0_xattn_bo"],
        "wg": i["L0_ffn_Wg"],
        "bg": i["L0_ffn_bg"],
        "wffn": np.concatenate([e13.transpose(1, 0, 2, 3).reshape(P, E, 2 * F), e2.reshape(P, E, FC * D)], axis=2),
    }
    arrays = {k: np.ascontiguousarray(a) for k, a in arrays.items()}
    nc = bacc.Bacc("TRN2", target_bir_lowering=False, num_devices=1)
    args = [nc.dram_tensor(k, a.shape, mybir.dt.from_np(a.dtype), kind="ExternalInput").ap() for k, a in arrays.items()]
    args.append(nc.dram_tensor("out", (B, T, D), F32, kind="ExternalOutput").ap())
    bass_xattn_moe(nc, *args)
    r = run_bass_kernel_spmd(nc, [arrays], core_ids=[0])
    return r.results[0]["out"]
```
